# Optimizing a Trainium2 kernel written in Bass

```python
import numpy as np
import jax
import jax.numpy as jnp

def _softmax(x, axis=-1):
    return jax.nn.softmax(x, axis=axis)

def _gelu(x):
    return jax.nn.gelu(x, approximate=True)

def _silu(x):
    return jax.nn.silu(x)

def _sigmoid(x):
    return jax.nn.sigmoid(x)

def _layernorm(x, axis=-1, eps=1e-05):
    m = jnp.mean(x, axis=axis, keepdims=True)
    v = jnp.var(x, axis=axis, keepdims=True)
    return (x - m) / jnp.sqrt(v + eps)

def _scatter_add(tgt, idx, src, axis=0):
    return tgt.at[idx].add(src)

def _segment_sum(src, seg, n):
    return jax.ops.segment_sum(src, seg, n)
kernel_name = 'mk_lm_tower_d1_tok_ids512_r4_60e75c'

def setup_inputs(seed: int=0):
    np.random.seed(seed)
    _w = jnp.asarray

    def _rec_inputs():
        import jax
        import jax.numpy as jnp
        _rk = jax.random.key(seed)
        x = jax.random.randint(jax.random.fold_in(_rk, 1), (32, 128), 0, 668, jnp.int32)
        return x
    x = _rec_inputs()

    def _L0_tok_setup():
        import jax, jax.numpy as jnp
        import numpy as np
        import math
        D = 128
        CAT_VOCAB = 128
        TIME_START, TIME_STEPS = (128, 250)
        NOTE_START, NOTE_RANGE = (378, 128)
        VEL_START, VEL_BINS = (410, 32)
        DUR_START, DUR_STEPS = (418, 250)
        VOCAB = 668

        def _time2vec(t, max_steps, lin_w, lin_b, w, b):
            tn = t.astype(jnp.float32)[..., None] / max_steps
            linear = tn * lin_w + lin_b
            periodic = jnp.sin(tn * w + b)
            return jnp.concatenate([linear, periodic], axis=-1)

        def _pitch_embed(p):
            pf = p.astype(jnp.float32)
            octave = jnp.floor(pf / 12.0)
            semitone = jnp.mod(pf, 12.0)
            i = jnp.arange(D // 4, dtype=jnp.float32)
            div = 2.0 ** i
            ph_oct = octave[..., None] / div
            ph_sem = semitone[..., None] * (math.pi / 6.0) * (i + 1.0)
            emb = jnp.stack([jnp.sin(ph_oct), jnp.cos(ph_oct), jnp.sin(ph_sem), jnp.cos(ph_sem)], axis=-1)
            return emb.reshape(*p.shape, D)

        def _vel_embed(v, w1, b1, w2, b2, g, beta):
            vn = v.astype(jnp.float32)[..., None] / VEL_BINS
            h = jax.nn.gelu(vn * w1 + b1, approximate=False)
            e = jnp.einsum('bsh,dh->bsd', h, w2) + b2
            mu = e.mean(-1, keepdims=True)
            var = ((e - mu) ** 2).mean(-1, keepdims=True)
            return g * (e - mu) / jnp.sqrt(var + 1e-05) + beta
        key = jax.random.key(seed)
        ks = jax.random.split(key, 16)
        tokens = jax.random.randint(ks[0], (8, 2048), 0, VOCAB)
        token_emb = jax.random.normal(ks[1], (CAT_VOCAB, D), jnp.float32) * 0.02
        token_emb = token_emb.at[0].set(0.0)
        return {'tokens': tokens, 'token_emb': token_emb, 'time_lin_w': jax.random.normal(ks[2], (D // 2,), jnp.float32), 'time_lin_b': jax.random.normal(ks[3], (D // 2,), jnp.float32), 'time_w': jax.random.normal(ks[4], (D // 2,), jnp.float32), 'time_b': jax.random.normal(ks[5], (D // 2,), jnp.float32), 'vel_w1': jax.random.normal(ks[6], (D // 2,), jnp.float32), 'vel_b1': jax.random.normal(ks[7], (D // 2,), jnp.float32), 'vel_w2': jax.random.normal(ks[8], (D, D // 2), jnp.float32) * 0.05, 'vel_b2': jax.random.normal(ks[9], (D,), jnp.float32), 'vel_ln_g': jnp.ones((D,), jnp.float32), 'vel_ln_b': jnp.zeros((D,), jnp.float32), 'dur_lin_w': jax.random.normal(ks[10], (D // 2,), jnp.float32), 'dur_lin_b': jax.random.normal(ks[11], (D // 2,), jnp.float32), 'dur_w': jax.random.normal(ks[12], (D // 2,), jnp.float32), 'dur_b': jax.random.normal(ks[13], (D // 2,), jnp.float32)}
    _L0_tok_all = _L0_tok_setup()
    _L0_tok_in = {k: v for k, v in _L0_tok_all.items() if k in ('token_emb', 'time_lin_w', 'time_lin_b', 'time_w', 'time_b', 'vel_w1', 'vel_b1', 'vel_w2', 'vel_b2', 'vel_ln_g', 'vel_ln_b', 'dur_lin_w', 'dur_lin_b', 'dur_w', 'dur_b')}
    del _L0_tok_all

    def _L0_attn_setup():
        import math
        import jax, jax.numpy as jnp
        import numpy as np
        DIM = 128
        HEADS = 8
        LS = 64
        SCALE = (DIM // HEADS) ** (-0.5)

        def _normalize(x, eps=1e-12):
            n = jnp.linalg.norm(x, axis=-1, keepdims=True)
            return x / jnp.maximum(n, eps)
        key = jax.random.key(seed)
        k0, k1, k2 = jax.random.split(key, 3)
        B, S, D = (8, 1024, DIM)
        return {'x': jax.random.normal(k0, (B, S, D), jnp.float32), 'W_qkv': jax.random.normal(k1, (D, 3 * D), jnp.float32) * 0.02, 'b_qkv': jnp.zeros((3 * D,), jnp.float32), 'W_proj': jax.random.normal(k2, (D, D), jnp.float32) * 0.02, 'b_proj': jnp.zeros((D,), jnp.float32)}
    _L0_attn_all = _L0_attn_setup()
    _L0_attn_in = {k: v for k, v in _L0_attn_all.items() if k in ('W_qkv', 'b_qkv', 'W_proj', 'b_proj')}
    del _L0_attn_all

    def _L0_ffn_setup():
        import jax, jax.numpy as jnp
        import numpy as np
        B, S, D, F, E = (4, 512, 128, 512, 8)
        key = jax.random.key(seed)
        k = jax.random.split(key, 5)
        x = jax.random.normal(k[0], (B, S, D), dtype=jnp.float32)
        Ws = jax.random.normal(k[1], (D, E), dtype=jnp.float32) * 0.02
        bs = jnp.zeros((E,), dtype=jnp.float32)
        W1 = jax.random.normal(k[2], (E, D, F), dtype=jnp.float32) * 0.02
        b1 = jnp.zeros((E, F), dtype=jnp.float32)
        W2 = jax.random.normal(k[3], (E, F, D), dtype=jnp.float32) * 0.02
        b2 = jnp.zeros((E, D), dtype=jnp.float32)
        return {'x': x, 'Ws': Ws, 'bs': bs, 'W1': W1, 'b1': b1, 'W2': W2, 'b2': b2}
    _L0_ffn_all = _L0_ffn_setup()
    _L0_ffn_in = {k: v for k, v in _L0_ffn_all.items() if k in ('Ws', 'bs', 'W1', 'b1', 'W2', 'b2')}
    del _L0_ffn_all
    return {'x': x, 'L0_tok_token_emb': _L0_tok_in['token_emb'], 'L0_tok_time_lin_w': _L0_tok_in['time_lin_w'], 'L0_tok_time_lin_b': _L0_tok_in['time_lin_b'], 'L0_tok_time_w': _L0_tok_in['time_w'], 'L0_tok_time_b': _L0_tok_in['time_b'], 'L0_tok_vel_w1': _L0_tok_in['vel_w1'], 'L0_tok_vel_b1': _L0_tok_in['vel_b1'], 'L0_tok_vel_w2': _L0_tok_in['vel_w2'], 'L0_tok_vel_b2': _L0_tok_in['vel_b2'], 'L0_tok_vel_ln_g': _L0_tok_in['vel_ln_g'], 'L0_tok_vel_ln_b': _L0_tok_in['vel_ln_b'], 'L0_tok_dur_lin_w': _L0_tok_in['dur_lin_w'], 'L0_tok_dur_lin_b': _L0_tok_in['dur_lin_b'], 'L0_tok_dur_w': _L0_tok_in['dur_w'], 'L0_tok_dur_b': _L0_tok_in['dur_b'], 'L0_attn_W_qkv': _L0_attn_in['W_qkv'], 'L0_attn_b_qkv': _L0_attn_in['b_qkv'], 'L0_attn_W_proj': _L0_attn_in['W_proj'], 'L0_attn_b_proj': _L0_attn_in['b_proj'], 'L0_ffn_Ws': _L0_ffn_in['Ws'], 'L0_ffn_bs': _L0_ffn_in['bs'], 'L0_ffn_W1': _L0_ffn_in['W1'], 'L0_ffn_b1': _L0_ffn_in['b1'], 'L0_ffn_W2': _L0_ffn_in['W2'], 'L0_ffn_b2': _L0_ffn_in['b2']}

def reference(x, L0_tok_token_emb, L0_tok_time_lin_w, L0_tok_time_lin_b, L0_tok_time_w, L0_tok_time_b, L0_tok_vel_w1, L0_tok_vel_b1, L0_tok_vel_w2, L0_tok_vel_b2, L0_tok_vel_ln_g, L0_tok_vel_ln_b, L0_tok_dur_lin_w, L0_tok_dur_lin_b, L0_tok_dur_w, L0_tok_dur_b, L0_attn_W_qkv, L0_attn_b_qkv, L0_attn_W_proj, L0_attn_b_proj, L0_ffn_Ws, L0_ffn_bs, L0_ffn_W1, L0_ffn_b1, L0_ffn_W2, L0_ffn_b2):
    import jax
    import jax.numpy as jnp

    def _L0_tok_ref(tokens, token_emb, time_lin_w, time_lin_b, time_w, time_b, vel_w1, vel_b1, vel_w2, vel_b2, vel_ln_g, vel_ln_b, dur_lin_w, dur_lin_b, dur_w, dur_b):
        import jax, jax.numpy as jnp
        import numpy as np
        import math
        D = 128
        CAT_VOCAB = 128
        TIME_START, TIME_STEPS = (128, 250)
        NOTE_START, NOTE_RANGE = (378, 128)
        VEL_START, VEL_BINS = (410, 32)
        DUR_START, DUR_STEPS = (418, 250)
        VOCAB = 668

        def _time2vec(t, max_steps, lin_w, lin_b, w, b):
            tn = t.astype(jnp.float32)[..., None] / max_steps
            linear = tn * lin_w + lin_b
            periodic = jnp.sin(tn * w + b)
            return jnp.concatenate([linear, periodic], axis=-1)

        def _pitch_embed(p):
            pf = p.astype(jnp.float32)
            octave = jnp.floor(pf / 12.0)
            semitone = jnp.mod(pf, 12.0)
            i = jnp.arange(D // 4, dtype=jnp.float32)
            div = 2.0 ** i
            ph_oct = octave[..., None] / div
            ph_sem = semitone[..., None] * (math.pi / 6.0) * (i + 1.0)
            emb = jnp.stack([jnp.sin(ph_oct), jnp.cos(ph_oct), jnp.sin(ph_sem), jnp.cos(ph_sem)], axis=-1)
            return emb.reshape(*p.shape, D)

        def _vel_embed(v, w1, b1, w2, b2, g, beta):
            vn = v.astype(jnp.float32)[..., None] / VEL_BINS
            h = jax.nn.gelu(vn * w1 + b1, approximate=False)
            e = jnp.einsum('bsh,dh->bsd', h, w2) + b2
            mu = e.mean(-1, keepdims=True)
            var = ((e - mu) ** 2).mean(-1, keepdims=True)
            return g * (e - mu) / jnp.sqrt(var + 1e-05) + beta
        cat_mask = tokens < CAT_VOCAB
        time_mask = (tokens >= TIME_START) & (tokens < TIME_START + TIME_STEPS)
        note_mask = (tokens >= NOTE_START) & (tokens < NOTE_START + NOTE_RANGE)
        vel_mask = (tokens >= VEL_START) & (tokens < VEL_START + VEL_BINS)
        dur_mask = (tokens >= DUR_START) & (tokens < DUR_START + DUR_STEPS)
        safe_idx = jnp.clip(tokens, 0, CAT_VOCAB - 1)
        out = jnp.where(cat_mask[..., None], token_emb[safe_idx], 0.0)
        t_emb = _time2vec(tokens - TIME_START, float(TIME_STEPS), time_lin_w, time_lin_b, time_w, time_b)
        p_emb = _pitch_embed(tokens - NOTE_START)
        v_emb = _vel_embed(tokens - VEL_START, vel_w1, vel_b1, vel_w2, vel_b2, vel_ln_g, vel_ln_b)
        d_emb = _time2vec(tokens - DUR_START, float(DUR_STEPS), dur_lin_w, dur_lin_b, dur_w, dur_b)
        out = jnp.where(time_mask[..., None], t_emb, out)
        out = jnp.where(note_mask[..., None], p_emb, out)
        out = jnp.where(vel_mask[..., None], v_emb, out)
        out = jnp.where(dur_mask[..., None], d_emb, out)
        return out

    def _L0_attn_ref(x, W_qkv, b_qkv, W_proj, b_proj):
        import math
        import jax, jax.numpy as jnp
        import numpy as np
        DIM = 128
        HEADS = 8
        LS = 64
        SCALE = (DIM // HEADS) ** (-0.5)

        def _normalize(x, eps=1e-12):
            n = jnp.linalg.norm(x, axis=-1, keepdims=True)
            return x / jnp.maximum(n, eps)
        B, S, D = x.shape
        H = HEADS
        d = D // H
        ls = LS
        nl = S // ls
        ntimes = int(math.log2(nl))
        qkv = (x @ W_qkv + b_qkv).reshape(B, S, 3, H, d).transpose(2, 0, 3, 1, 4)
        q_pre = qkv[0].reshape(B * H, S, d).transpose(0, 2, 1)
        q_idx_last = jnp.broadcast_to(jnp.arange(S)[None, :], (B * H, S))
        for _ in range(ntimes):
            bh, dd, n = q_pre.shape
            q_avg = q_pre.reshape(bh, dd, 2, n // 2).mean(-1)
            q_avg = _normalize(q_avg.transpose(0, 2, 1))
            q_norm = _normalize(q_pre.transpose(0, 2, 1))
            sq = jnp.sum(q_norm ** 2, -1)[:, :, None] + jnp.sum(q_avg ** 2, -1)[:, None, :] - 2.0 * jnp.einsum('bnd,bcd->bnc', q_norm, q_avg)
            q_ratio = (sq[:, :, 0] + 1.0) / (sq[:, :, 1] + 1.0)
            q_idx = jnp.argsort(q_ratio, axis=-1)
            q_idx_last = jnp.take_along_axis(q_idx_last, q_idx, axis=-1).reshape(bh * 2, n // 2)
            q_pre = jnp.take_along_axis(q_pre, q_idx[:, None, :], axis=-1)
            q_pre = q_pre.reshape(bh, dd, 2, n // 2).transpose(0, 2, 1, 3).reshape(bh * 2, dd, n // 2)
        q_idx = q_idx_last.reshape(B, H, S)
        q_idx_rev = jnp.argsort(q_idx, axis=-1)
        qkv_pre = jnp.take_along_axis(qkv, q_idx[None, :, :, :, None], axis=3)
        qkv_pre = qkv_pre.reshape(3, B, H, nl, ls, d).transpose(0, 1, 3, 2, 4, 5).reshape(3, B * nl, H, ls, d)
        q, k, v = (qkv_pre[0], qkv_pre[1], qkv_pre[2])
        attn = jax.nn.softmax((q - k) * SCALE, axis=-1)
        out = attn * v
        out = out.reshape(B, nl, H, ls, d).transpose(0, 2, 4, 1, 3).reshape(B, H, d, S)
        out = jnp.take_along_axis(out, q_idx_rev[:, :, None, :], axis=-1)
        res = out.reshape(B, D, S).transpose(0, 2, 1)
        res = res @ W_proj + b_proj
        return x + res

    def _L0_ffn_ref(x, Ws, bs, W1, b1, W2, b2):
        import jax, jax.numpy as jnp
        import numpy as np
        B, S, D, F, E = (4, 512, 128, 512, 8)
        Bb, Ss, Dd = x.shape
        xt = x.reshape(-1, Dd)
        logits = xt @ Ws + bs
        probs = jax.nn.softmax(logits, axis=-1)
        prob_max = jnp.max(probs, axis=-1)
        routes = jnp.argmax(probs, axis=-1)
        onehot = jax.nn.one_hot(routes, W1.shape[0], dtype=xt.dtype)

        def expert_ffn(w1, bb1, w2, bb2):
            h = jax.nn.gelu(xt @ w1 + bb1, approximate=False)
            return h @ w2 + bb2
        y = jax.vmap(expert_ffn)(W1, b1, W2, b2)
        out = jnp.einsum('te,etd->td', onehot, y)
        out = out * prob_max[:, None]
        return out.reshape(Bb, Ss, Dd)
    h = _L0_tok_ref(x, L0_tok_token_emb, L0_tok_time_lin_w, L0_tok_time_lin_b, L0_tok_time_w, L0_tok_time_b, L0_tok_vel_w1, L0_tok_vel_b1, L0_tok_vel_w2, L0_tok_vel_b2, L0_tok_vel_ln_g, L0_tok_vel_ln_b, L0_tok_dur_lin_w, L0_tok_dur_lin_b, L0_tok_dur_w, L0_tok_dur_b)
    h = h + _L0_attn_ref(_layernorm(h, axis=-1), L0_attn_W_qkv, L0_attn_b_qkv, L0_attn_W_proj, L0_attn_b_proj)
    h = h + _L0_ffn_ref(_layernorm(h, axis=-1), L0_ffn_Ws, L0_ffn_bs, L0_ffn_W1, L0_ffn_b1, L0_ffn_W2, L0_ffn_b2)
    return h

_drawn_inputs = setup_inputs


def setup_inputs(seed=0):
    import zlib

    import numpy as np

    out = dict(_drawn_inputs(seed))
    spreads = {'L0_tok_vel_ln_g': (1.0, 0.6),
     'L0_tok_vel_ln_b': (0.0, 0.682),
     'L0_attn_b_qkv': (0.0, 0.8),
     'L0_attn_b_proj': (0.0, 0.1),
     'L0_ffn_bs': (0.0, 0.8),
     'L0_ffn_b1': (0.0, 0.8),
     'L0_ffn_b2': (0.0, 0.8)}
    factors = {'L0_tok_vel_w1': 23.771,
     'L0_attn_W_qkv': 8.0,
     'L0_attn_W_proj': 8.0,
     'L0_ffn_Ws': 5.109,
     'L0_ffn_W1': 8.0,
     'L0_ffn_W2': 8.0}
    for name, (base, spread) in spreads.items():
        noise = np.random.default_rng([zlib.crc32(name.encode()), seed]).standard_normal(out[name].shape)
        drawn = base * np.exp(spread * noise) if base else spread * noise
        out[name] = jnp.asarray(drawn.astype(out[name].dtype))
    for name, factor in factors.items():
        out[name] = (out[name] * factor).astype(out[name].dtype)
    return out
```

```python
from contextlib import ExitStack

import concourse.bass as bass
import numpy as np
from concourse import mybir

ALU = mybir.AluOpType
ACT = mybir.ActivationFunctionType
AX = mybir.AxisListType
F32 = mybir.dt.float32
I32 = mybir.dt.int32
U32 = mybir.dt.uint32

P = 128
D = 128
H = 8
DH = D // H
HALF = D // 2
E = 8
F = 512
FC = F // P
TOKENS = 32 * 128
CAT, TIME0, NOTE0, VEL0, DUR0, VOCAB = 128, 128, 378, 410, 418, 668
TIME_STEPS = DUR_STEPS = 250
VEL_BINS = 32
ROWS = VOCAB + 1
TILES = -(-ROWS // P)
LAST = ROWS - (TILES - 1) * P
PAIRS = TILES // 2
NOTES_AND_VEL = VEL0 // P
VEL_AT = VEL0 % P
N_VEL = DUR0 - VEL0
EPS = 1e-5
SCALE = DH ** -0.5
JOBS = TOKENS // P

TWO_PI = (6.28125, 0.0019350051879882812, 3.019915981956753e-07)
PI_BELOW = float(np.float32(3.1415925))
ROUND = 1.5 * 2.0 ** 23
RSQRT_SEED = float(0x5F3759DF)
PHASE_ROWS = 7


def vocabulary_rows():
    v = np.arange(TILES * P)
    rows = np.zeros((PHASE_ROWS, TILES * P), np.float32)
    time = (v >= TIME0) & (v < NOTE0)
    note = (v >= NOTE0) & (v < VEL0)
    dur = (v >= DUR0) & (v < VOCAB)
    rows[0, time] = (v[time] - TIME0).astype(np.float32) / np.float32(TIME_STEPS)
    rows[1, time] = 1.0
    rows[2, dur] = (v[dur] - DUR0).astype(np.float32) / np.float32(DUR_STEPS)
    rows[3, dur] = 1.0
    rows[4, note] = (v[note] - NOTE0) // 12
    rows[5, note] = (v[note] - NOTE0) % 12
    rows[6, note] = 1.0
    return rows[:, P:]


def pitch_rows():
    i = np.arange(D // 4)
    rows = np.zeros((3, D), np.float32)
    rows[0, 0::4] = rows[0, 1::4] = 2.0 ** -i
    rows[1, 2::4] = rows[1, 3::4] = np.float32(np.pi / 6) * (i + 1)
    rows[2, 1::2] = np.pi / 2
    return rows


def build(nc, x, phases, vel, vel_scale, consts, token_emb, weights, rows, w1, w2, b2, out):
    table = nc.dram_tensor("table", [TILES * P, D], F32)
    with ExitStack() as ctx:
        def sb(name, shape, dt=F32):
            return ctx.enter_context(nc.sbuf_tensor(name, shape, dt))

        def sem(name):
            return ctx.enter_context(nc.semaphore(name))

        tok_in = sb("tok_in", [P, JOBS], I32)
        tok = sb("tok", [P, JOBS], U32)
        ph_in = sb("ph_in", [PHASE_ROWS, (TILES - 1) * P + HALF + D])
        row_basis = ph_in[:, 0:(TILES - 1) * P]
        lin_cols = ph_in[:, (TILES - 1) * P:(TILES - 1) * P + HALF]
        sin_cols = ph_in[:, (TILES - 1) * P + HALF:]
        vel_in = sb("vel_in", [HALF + 1, 2 * P + 2 + N_VEL])
        vel_hid, vel_w2 = vel_in[:, 0:P], vel_in[:, P:2 * P]
        vel_w1, vel_b1 = vel_in[0:HALF, 2 * P:2 * P + 1], vel_in[0:HALF, 2 * P + 1:2 * P + 2]
        vel_n = vel_in[0:HALF, 2 * P + 2:]
        vel_gb = sb("vel_gb", [P, 2, D])
        con = sb("con", [P, 2, P])
        ident = con[:, 0, :]
        w = sb("w", [P, 3 * D + D + E])
        w_proj, w_gate = w[:, 3 * D:4 * D], w[:, 4 * D:]
        rw = sb("rw", [1, 3 * D + D + E])
        b_proj, b_gate = rw[:, 3 * D:4 * D], rw[:, 4 * D:]
        w1_sb = sb("w1_sb", [P, E, F + FC])
        w2_sb = sb("w2_sb", [P, E, FC, D])
        b2_sb = sb("b2_sb", [1, E, D])
        ones = sb("ones", [1, P])
        h = sb("h", [P, TILES, D])
        h_half = h.rearrange("p t (a n) -> p (t a) n", a=2)
        turns = sb("turns", [P, 7, HALF])
        ang = sb("ang", [P, 7, HALF])
        stats = sb("stats", [P, TILES + 1, 6])
        mv = sb("mv", [P, TILES + 1, 2])
        ve = sb("ve", [P, TILES + 1, 1])
        seed = sb("seed", [P, TILES + 1, 1], I32)
        rstd = sb("rstd", [P, TILES + 1, 1])
        sq = sb("sq", [P, TILES + 1, 1])
        vn = sb("vn", [P, D])
        x1 = sb("x1", [P, TILES, D])
        x1T = sb("x1T", [P, TILES, P])
        hx = sb("hx", [P, TILES, D])
        wz = sb("wz", [P, D])
        bz = sb("bz", [1, D])
        zmax = sb("zmax", [P, TILES, H, 1])
        zs = sb("zs", [P, TILES, D])
        prob = sb("prob", [P, TILES, D])
        zsum = sb("zsum", [P, TILES, H, 1])
        zrec = sb("zrec", [P, TILES, H, 1])
        pv = sb("pv", [P, TILES, D])
        att = sb("att", [P, TILES, D])
        attT = sb("attT", [P, TILES, P])
        h2 = sb("h2", [P, TILES, D])
        x2 = sb("x2", [P, TILES, D])
        x2T = sb("x2T", [P, TILES, P])
        lmax = sb("lmax", [P, TILES, 1])
        lshift = sb("lshift", [P, TILES, E])
        lexp = sb("lexp", [P, TILES, E])
        lsum = sb("lsum", [P, TILES, 1])
        pmax = sb("pmax", [P, TILES, 1])
        best = sb("best", [P, TILES, E])
        rank = sb("rank", [P, E])
        order = sb("order", [P, TILES, E])
        omax = sb("omax", [P, TILES, 1])
        onehot = sb("onehot", [P, TILES, E])
        hid = sb("hid", [P, 2, FC, TILES * P])
        acc = sb("acc", [P, TILES, D])
        tab = sb("tab", [P, TILES, D])
        got = sb("got", [P, JOBS, D])

        psum = [ctx.enter_context(nc.psum_tensor(f"bank{i}", [P, 512], F32)) for i in range(0)]
        ps = ctx.enter_context(nc.psum_tensor("ps", [P, 8, 512], F32))
        ps_lin = ps[:, 0, 0:5 * HALF].rearrange("p (t n) -> p t n", n=HALF)
        ps_sin = ps[:, 1, 0:7 * HALF].rearrange("p (t n) -> p t n", n=HALF)
        ps_vel = ps[:, 2, 0:P]
        t128 = [(PAIRS + t // 2, t % 2 * P) for t in range(TILES)]
        a128 = t128
        o128 = [(b, 2 * P + n) for b, n in t128]

        def pair(at, g):
            b, o = at[2 * g]
            return ps[:, b, o:o + 2 * P].rearrange("p (t n) -> p t n", n=P)

        def tile(at, t):
            b, o = at[t]
            return ps[:, b, o:o + P]

        def zv(g):
            return ps[:, g, :].rearrange("p (t k n) -> p t k n", t=2, k=2)
        ps_gate = ps[:, 6, 0:TILES * E].rearrange("p (t e) -> p t e", e=E)
        ps_hid = [ps[:, 2 * i:2 * i + 2, :].rearrange("p b n -> p (b n)") for i in range(2)]
        ps_y = [ps[:, 4 + 2 * i:6 + 2 * i, :].rearrange("p b n -> p (b n)") for i in range(2)]

        s_tok = sem("s_tok")
        s_ph = sem("s_ph")
        s_vel = sem("s_vel")
        s_gb = sem("s_gb")
        s_con = sem("s_con")
        s_emb = sem("s_emb")
        s_w = sem("s_w")
        s_rw = sem("s_rw")
        s_w1 = sem("s_w1")
        s_w2 = sem("s_w2")
        s_b2 = sem("s_b2")
        ones_set = sem("ones_set")
        phases_done = sem("phases_done")
        vel_hidden = sem("vel_hidden")
        vel_out = sem("vel_out")
        angles_done = sem("angles_done")
        sines_done = sem("sines_done")
        dve_seq = sem("dve_seq")
        x1_done = sem("x1_done")
        x1T_ps = sem("x1T_ps")
        x1T_done = sem("x1T_done")
        wz_done = sem("wz_done")
        hx_done = sem("hx_done")
        zv_done = sem("zv_done")
        zs_done = sem("zs_done")
        exp_done = sem("exp_done")
        att_done = sem("att_done")
        attT_ps = sem("attT_ps")
        attT_done = sem("attT_done")
        o_done = sem("o_done")
        x2_done = sem("x2_done")
        x2T_ps = sem("x2T_ps")
        x2T_done = sem("x2T_done")
        gate_done = sem("gate_done")
        lshift_done = sem("lshift_done")
        lexp_done = sem("lexp_done")
        gate_read = sem("gate_read")
        hid_ps = sem("hid_ps")
        hid_done = sem("hid_done")
        y_done = sem("y_done")
        y_used = sem("y_used")
        tab_done = sem("tab_done")
        table_out = sem("table_out")
        tok_done = sem("tok_done")
        rows_got = [sem(f"rows_got{i}") for i in range(4)]
        out_done = sem("out_done")

        block = ctx.enter_context(nc.Block())

        @block.sync
        def _(sp):
            sp.dma_start(ph_in[:, :], phases[:, :]).then_inc(s_ph, 16)
            sp.dma_start(con[:, :, :], consts[:, :, :]).then_inc(s_con, 16)
            sp.dma_start(h[:, 0, :], token_emb[:, :]).then_inc(s_emb, 16)
            sp.dma_start(w[:, :], weights[:, :]).then_inc(s_w, 16)
            sp.dma_start(rw[:, :], rows[:, :]).then_inc(s_rw, 16)
            sp.dma_start(w1_sb[:, :, :], w1[:, :, :]).then_inc(s_w1, 16)
            sp.dma_start(w2_sb[:, :, :, :], w2[:, :, :, :]).then_inc(s_w2, 16)
            sp.dma_start(b2_sb[:, :, :], b2[:, :, :]).then_inc(s_b2, 16)
            sp.wait_ge(tab_done, 1)
            sp.dma_start(table.ap().rearrange("(t p) n -> p t n", p=P), tab[:, :, :]).then_inc(table_out, 16)
            for c in range(4):
                sp.wait_ge(rows_got[c], 8 * 16)
                sp.dma_start(out.rearrange("(p j) n -> p j n", p=P)[:, 8 * c:8 * c + 8, :],
                             got[:, 8 * c:8 * c + 8, :]).then_inc(out_done, 16)
            sp.wait_ge(out_done, 4 * 16)

        @block.gpsimd
        def _(pool):
            pool.memset(ones[:, :], 1.0).then_inc(ones_set, 1)
            pool.iota(rank[:, :], [[-1, E]], base=E, channel_multiplier=0,
                      allow_small_or_imprecise_dtypes=True).then_inc(ones_set, 1)
            for g in range(PAIRS):
                pool.wait_ge(x1_done, g + 1)
                pool.tensor_tensor(hx[:, 2 * g:2 * g + 2, :], h[:, 2 * g:2 * g + 2, :],
                                   x1[:, 2 * g:2 * g + 2, :], ALU.add).then_inc(hx_done, 1)
            pool.wait_ge(tok_done, 1)
            pool.wait_ge(table_out, 16)
            for j in range(JOBS):
                pool.indirect_dma_start(
                    out=got[:, j, :], out_offset=None, in_=table.ap()[:, :],
                    in_offset=bass.IndirectOffsetOnAxis(ap=tok[:, j:j + 1], axis=0)).then_inc(rows_got[j // 8], 16)

        @block.scalar
        def _(act):
            act.dma_start(vel_in[:, :], vel[:, :]).then_inc(s_vel, 16)
            act.dma_start(vel_gb[:, :, :], vel_scale[:, :, :]).then_inc(s_gb, 16)
            act.dma_start(tok_in[:, :], x[:, :]).then_inc(s_tok, 16)
            act.wait_ge(s_vel, 16)
            act.activation(vel_hid[0:HALF, VEL_AT:VEL_AT + N_VEL], vel_n, ACT.Gelu,
                           bias=vel_b1, scale=vel_w1).then_inc(vel_hidden, 1)
            act.wait_ge(phases_done, 1)
            act.activation(h_half[:, 2, :], ps_lin[:, 0, :], ACT.Copy)
            act.activation(h_half[:, 8:11:2, :], ps_lin[:, 3:5, :], ACT.Copy)
            act.wait_ge(angles_done, 1)
            act.activation(h_half[:, 3:8, :], ang[:, 0:5, :], ACT.Sin)
            act.activation(h_half[:, 9:12:2, :], ang[:, 5:7, :], ACT.Sin).then_inc(sines_done, 1)

            def x1T_copy(g):
                act.wait_ge(x1T_ps, g + 1)
                act.activation(x1T[:, 2 * g:2 * g + 2, :], pair(t128, g), ACT.Copy).then_inc(x1T_done, 1)

            def exps(g):
                act.wait_ge(zs_done, g + 1)
                act.activation(prob[:, 2 * g:2 * g + 2, :], zs[:, 2 * g:2 * g + 2, :], ACT.Exp,
                               scale=SCALE).then_inc(exp_done, 1)

            def attT_copy(g):
                act.wait_ge(attT_ps, g + 1)
                act.activation(attT[:, 2 * g:2 * g + 2, :], pair(a128, g), ACT.Copy).then_inc(attT_done, 1)

            def x2T_copy(g):
                act.wait_ge(x2T_ps, g + 1)
                act.activation(x2T[:, 2 * g:2 * g + 2, :], pair(t128, g), ACT.Copy).then_inc(x2T_done, 1)

            x1T_copy(0)
            x1T_copy(1)
            exps(0)
            x1T_copy(2)
            exps(1)
            attT_copy(0)
            exps(2)
            attT_copy(1)
            attT_copy(2)
            x2T_copy(0)
            x2T_copy(1)
            x2T_copy(2)
            act.wait_ge(lshift_done, 1)
            act.activation(lexp[:, :, :], lshift[:, :, :], ACT.Exp).then_inc(lexp_done, 1)
            n = 0
            for e in range(E):
                for c in range(FC):
                    n += 1
                    act.wait_ge(hid_ps, n)
                    if e >= 2:
                        act.wait_ge(y_done, e - 1)
                    act.activation(hid[:, e % 2, c, 0:ROWS], ps_hid[c % 2][:, 0:ROWS], ACT.Gelu,
                                   bias=w1_sb[:, e, F + c:F + c + 1]).then_inc(hid_done, 1)

        @block.tensor
        def _(pe):
            pe.wait_ge(s_ph, 16)
            for t in range(TILES - 1):
                lhs = row_basis[:, t * P:(t + 1) * P]
                pe.matmul(ps_lin[:, t, :], lhs, lin_cols, start=True, stop=True)
            for at, t, cols in ((0, 0, slice(HALF, D)), (1, 1, slice(0, D)), (3, 2, slice(0, D)),
                                (5, 3, slice(HALF, D)), (6, 4, slice(HALF, D))):
                n = cols.stop - cols.start
                mm = pe.matmul(ps[:, 1, at * HALF:at * HALF + n], row_basis[:, t * P:(t + 1) * P],
                               sin_cols[:, cols], start=True, stop=True)
            mm.then_inc(phases_done, 1)
            pe.wait_ge(vel_hidden, 1)
            pe.matmul(ps_vel, vel_hid, vel_w2, start=True, stop=True).then_inc(vel_out, 1)

            def x1_turn(g):
                pe.wait_ge(s_con, 16)
                pe.wait_ge(x1_done, g + 1)
                for t in (2 * g, 2 * g + 1):
                    mm = pe.transpose(tile(t128, t), x1[:, t, :], ident)
                mm.then_inc(x1T_ps, 1)

            def scores(g):
                if g == 0:
                    pe.wait_ge(s_w, 16)
                    pe.wait_ge(s_rw, 16)
                    pe.wait_ge(wz_done, 1)
                    pe.wait_ge(ones_set, 2)
                pe.wait_ge(x1T_done, g + 1)
                for t in (2 * g, 2 * g + 1):
                    for k, (wk, bk) in enumerate(((wz[:, :], bz[:, :]), (w[:, 2 * D:3 * D], rw[:, 2 * D:3 * D]))):
                        at = zv(g)[:, t % 2, k, :]
                        pe.matmul(at, ones[:, :], bk, start=True, stop=False)
                        mm = pe.matmul(at, x1T[:, t, :], wk, start=False, stop=True)
                mm.then_inc(zv_done, 1)

            def att_turn(g):
                pe.wait_ge(att_done, g + 1)
                for t in (2 * g, 2 * g + 1):
                    mm = pe.transpose(tile(a128, t), att[:, t, :], ident)
                mm.then_inc(attT_ps, 1)

            def project(g):
                pe.wait_ge(attT_done, g + 1)
                for t in (2 * g, 2 * g + 1):
                    pe.matmul(tile(o128, t), ones[:, :], b_proj, start=True, stop=False)
                    mm = pe.matmul(tile(o128, t), attT[:, t, :], w_proj, start=False, stop=True)
                mm.then_inc(o_done, 1)

            def x2_turn(g):
                pe.wait_ge(x2_done, g + 1)
                for t in (2 * g, 2 * g + 1):
                    mm = pe.transpose(tile(t128, t), x2[:, t, :], ident)
                mm.then_inc(x2T_ps, 1)

            def gate(g):
                pe.wait_ge(x2T_done, g + 1)
                for t in (2 * g, 2 * g + 1):
                    pe.matmul(ps_gate[:, t, :], ones[:, :], b_gate, start=True, stop=False)
                    mm = pe.matmul(ps_gate[:, t, :], x2T[:, t, :], w_gate, start=False, stop=True)
                if g == PAIRS - 1:
                    mm.then_inc(gate_done, 1)

            x1_turn(0)
            x1_turn(1)
            scores(0)
            x1_turn(2)
            scores(1)
            scores(2)
            att_turn(0)
            project(0)
            att_turn(1)
            project(1)
            att_turn(2)
            project(2)
            for g in range(PAIRS):
                x2_turn(g)
                gate(g)
            pe.wait_ge(s_w1, 16)
            pe.wait_ge(s_w2, 16)
            pe.wait_ge(s_b2, 16)
            pe.wait_ge(gate_read, 1)

            def up(e, c):
                n = e * FC + c
                if n >= 2:
                    pe.wait_ge(hid_done, n - 1)
                for a, b in ((0, 512), (512, ROWS)):
                    mm = pe.matmul(ps_hid[c % 2][:, a:b], w1_sb[:, e, c * P:(c + 1) * P],
                                   x2T.rearrange("p t n -> p (t n)")[:, a:b], start=True, stop=True)
                mm.then_inc(hid_ps, 1)

            def down(e):
                pe.wait_ge(hid_done, (e + 1) * FC)
                if e >= 2:
                    pe.wait_ge(y_used, e - 1)
                for t in range(TILES):
                    m = P if t < TILES - 1 else LAST
                    at = ps_y[e % 2][0:m, t * P:(t + 1) * P]
                    pe.matmul(at, ones[:, 0:m], b2_sb[:, e, :], start=True, stop=False)
                    for c in range(FC):
                        mm = pe.matmul(at, hid[:, e % 2, c, t * P:t * P + m], w2_sb[:, e, c, :],
                                       start=False, stop=(c == FC - 1))
                mm.then_inc(y_done, 1)
            for e in range(E + 1):
                if e < E:
                    for c in range(FC):
                        up(e, c)
                if e >= 1:
                    down(e - 1)

        @block.vector
        def _(dve):
            seq = [0]

            def then(ins):
                seq[0] += 1
                ins.then_inc(dve_seq, 1)
                dve.wait_ge(dve_seq, seq[0])

            def inverse_root(n, at):
                v, s, y, q = (a[0:n, at, :] for a in (ve, seed, rstd, sq))
                then(dve.tensor_scalar(v, mv[0:n, at, 1:2], EPS, None, ALU.add))
                then(dve.tensor_scalar(s, v.bitcast(I32), 1, None, ALU.logical_shift_right))
                then(dve.tensor_scalar(y.bitcast(I32), s, -1.0, RSQRT_SEED, ALU.mult, ALU.add))
                for _ in range(3):
                    then(dve.tensor_tensor(q, y, y, ALU.mult))
                    then(dve.scalar_tensor_tensor(q, q, -0.5, v, ALU.mult, ALU.mult))
                    then(dve.scalar_tensor_tensor(y, q, 1.5, y, ALU.add, ALU.mult))

            dve.memset(acc[:, :, :], 0.0)
            dve.wait_ge(s_tok, 16)
            dve.tensor_scalar(tok[:, :], tok_in[:, :], float(VOCAB), 0.0, ALU.min, ALU.max).then_inc(tok_done, 1)
            dve.wait_ge(phases_done, 1)
            then(dve.tensor_scalar(turns[:, :, :], ps_sin, 1.0 / (2 * np.pi), ROUND, ALU.mult, ALU.add))
            then(dve.tensor_scalar(turns[:, :, :], turns[:, :, :], ROUND, None, ALU.subtract))
            then(dve.scalar_tensor_tensor(ang[:, :, :], turns[:, :, :], -TWO_PI[0], ps_sin, ALU.mult, ALU.add))
            then(dve.scalar_tensor_tensor(ang[:, :, :], turns[:, :, :], -TWO_PI[1], ang[:, :, :], ALU.mult, ALU.add))
            then(dve.scalar_tensor_tensor(ang[:, :, :], turns[:, :, :], -TWO_PI[2], ang[:, :, :], ALU.mult, ALU.add))
            dve.tensor_scalar(ang[:, :, :], ang[:, :, :], PI_BELOW, -PI_BELOW, ALU.min, ALU.max).then_inc(angles_done, 1)
            n = HALF
            dve.wait_ge(vel_out, 1)
            then(dve.bn_stats(stats[0:n, TILES, :], ps_vel[0:n, :]))
            then(dve.bn_aggr(mv[0:n, TILES, :], stats[0:n, TILES, :]))
            inverse_root(n, slice(TILES, TILES + 1))
            then(dve.tensor_scalar(vn[0:n, :], ps_vel[0:n, :], mv[0:n, TILES, 0:1], rstd[0:n, TILES, :],
                                   ALU.subtract, ALU.mult))
            dve.wait_ge(s_gb, 16)
            then(dve.tensor_tensor(vn[0:n, :], vn[0:n, :], vel_gb[0:n, 0, :], ALU.mult))
            then(dve.tensor_tensor(vn[0:n, :], vn[0:n, :], vel_gb[0:n, 1, :], ALU.add))
            dve.wait_ge(s_w, 16)
            dve.wait_ge(s_rw, 16)
            dve.tensor_tensor(wz[:, :], w[:, 0:D], w[:, D:2 * D], ALU.subtract)
            dve.tensor_tensor(bz[:, :], rw[:, 0:D], rw[:, D:2 * D], ALU.subtract).then_inc(wz_done, 1)
            dve.wait_ge(sines_done, 1)
            then(dve.tensor_tensor(h_half[:, 4:7:2, :], h_half[:, 4:7:2, :], ps_lin[:, 1:3, :], ALU.add))
            t = NOTES_AND_VEL
            then(dve.tensor_tensor(h[0:n, t, :], h[0:n, t, :], vn[0:n, :], ALU.add))
            dve.wait_ge(s_emb, 16)

            def norm(g, src, dst, done):
                a = slice(2 * g, 2 * g + 2)
                for t in (2 * g, 2 * g + 1):
                    ins = dve.bn_stats(stats[:, t, :], src[:, t, :])
                then(ins)
                for t in (2 * g, 2 * g + 1):
                    ins = dve.bn_aggr(mv[:, t, :], stats[:, t, :])
                then(ins)
                inverse_root(P, a)
                for t in (2 * g, 2 * g + 1):
                    ins = dve.tensor_scalar(dst[:, t, :], src[:, t, :], mv[:, t, 0:1], rstd[:, t, :],
                                            ALU.subtract, ALU.mult)
                ins.then_inc(done, 1)

            def heads(ap):
                return ap.rearrange("p t (h d) -> p t h d", d=DH)

            def wide(ap):
                return ap.broadcast_to([P, 2, H, DH])

            def shift(g):
                a = slice(2 * g, 2 * g + 2)
                dve.wait_ge(zv_done, g + 1)
                z = heads(zv(g)[:, :, 0, :])
                then(dve.tensor_reduce(zmax[:, a, :, :], z, AX.X, ALU.max))
                dve.tensor_tensor(heads(zs[:, a, :]), z, wide(zmax[:, a, :, :]), ALU.subtract).then_inc(zs_done, 1)

            def weigh(g):
                a = slice(2 * g, 2 * g + 2)
                dve.wait_ge(exp_done, g + 1)
                dve.tensor_tensor(pv[:, a, :], prob[:, a, :], zv(g)[:, :, 1, :], ALU.mult)
                then(dve.tensor_reduce(zsum[:, a, :, :], heads(prob[:, a, :]), AX.X, ALU.add))
                then(dve.reciprocal(zrec[:, a, :, :], zsum[:, a, :, :]))
                dve.tensor_tensor(heads(att[:, a, :]), heads(pv[:, a, :]), wide(zrec[:, a, :, :]),
                                  ALU.mult).then_inc(att_done, 1)

            def norm2(g):
                dve.wait_ge(o_done, g + 1)
                dve.wait_ge(hx_done, g + 1)
                a = slice(2 * g, 2 * g + 2)
                then(dve.tensor_tensor(h2[:, a, :], hx[:, a, :], pair(o128, g), ALU.add))
                norm(g, h2, x2, x2_done)

            norm(0, h, x1, x1_done)
            norm(1, h, x1, x1_done)
            shift(0)
            norm(2, h, x1, x1_done)
            shift(1)
            weigh(0)
            shift(2)
            weigh(1)
            norm2(0)
            weigh(2)
            norm2(1)
            norm2(2)
            dve.wait_ge(gate_done, 1)
            then(dve.tensor_reduce(lmax[:, :, :], ps_gate, AX.X, ALU.max))
            wide_max = lmax[:, :, :].broadcast_to([P, TILES, E])
            dve.tensor_tensor(lshift[:, :, :], ps_gate, wide_max, ALU.subtract).then_inc(lshift_done, 1)
            dve.wait_ge(ones_set, 2)
            dve.tensor_tensor(best[:, :, :], ps_gate, wide_max, ALU.is_equal).then_inc(gate_read, 1)
            dve.wait_ge(gate_read, 1)
            then(dve.tensor_tensor(order[:, :, :], best[:, :, :],
                                   rank.rearrange("p (a e) -> p a e", a=1).broadcast_to([P, TILES, E]), ALU.mult))
            then(dve.tensor_reduce(omax[:, :, :], order[:, :, :], AX.X, ALU.max))
            then(dve.tensor_tensor(onehot[:, :, :], order[:, :, :], omax[:, :, :].broadcast_to([P, TILES, E]),
                                   ALU.is_equal))
            dve.wait_ge(lexp_done, 1)
            then(dve.tensor_reduce(lsum[:, :, :], lexp[:, :, :], AX.X, ALU.add))
            then(dve.reciprocal(pmax[:, :, :], lsum[:, :, :]))
            for e in range(E):
                dve.wait_ge(y_done, e + 1)
                for t in range(TILES):
                    m = P if t < TILES - 1 else LAST
                    ins = dve.scalar_tensor_tensor(acc[0:m, t, :], ps_y[e % 2][0:m, t * P:(t + 1) * P],
                                                   onehot[0:m, t, e:e + 1], acc[0:m, t, :], ALU.mult, ALU.add)
                ins.then_inc(y_used, 1)
                dve.wait_ge(y_used, e + 1)
            for t in range(TILES):
                ins = dve.scalar_tensor_tensor(tab[:, t, :], acc[:, t, :], pmax[:, t, :], h2[:, t, :],
                                               ALU.mult, ALU.add)
            ins.then_inc(tab_done, 1)


def kernel(**inputs):
    import numpy as _np
    import concourse.bacc as _bacc
    from concourse.bass_utils import run_bass_kernel_spmd as _run

    a = {k.removeprefix("L0_"): _np.asarray(v) for k, v in inputs.items()}
    f32 = _np.float32

    sines = _np.zeros((PHASE_ROWS, HALF + D), f32)
    for k, name in enumerate(("time_lin_w", "time_lin_b", "dur_lin_w", "dur_lin_b")):
        sines[k, 0:HALF] = a["tok_" + name]
    for k, name in enumerate(("time_w", "time_b", "dur_w", "dur_b")):
        sines[k, HALF + HALF:] = a["tok_" + name]
    sines[4:, HALF:] = pitch_rows()

    vel = _np.zeros((HALF + 1, 2 * P + 2 + N_VEL), f32)
    vel[HALF, VEL_AT:VEL_AT + N_VEL] = 1.0
    vel[0:HALF, P:2 * P] = a["tok_vel_w2"].T
    vel[HALF, P:2 * P] = a["tok_vel_b2"]
    vel[0:HALF, 2 * P] = a["tok_vel_w1"]
    vel[0:HALF, 2 * P + 1] = a["tok_vel_b1"]
    vel[:, 2 * P + 2:] = _np.arange(N_VEL, dtype=f32) / f32(VEL_BINS)
    vel_scale = _np.zeros((P, 2, D), f32)
    vel_scale[VEL_AT:VEL_AT + N_VEL, 0] = a["tok_vel_ln_g"]
    vel_scale[VEL_AT:VEL_AT + N_VEL, 1] = a["tok_vel_ln_b"]

    w1 = _np.zeros((P, E, F + FC), f32)
    w1[:, :, 0:F] = a["ffn_W1"].transpose(1, 0, 2)
    w1[:, :, F:] = a["ffn_b1"].reshape(E, FC, P).transpose(2, 0, 1)
    arrays = {
        "x": a["x"].reshape(P, JOBS),
        "phases": _np.concatenate([vocabulary_rows(), sines], 1),
        "vel": vel,
        "vel_scale": vel_scale,
        "consts": _np.stack([_np.eye(P, dtype=f32), _np.triu(_np.ones((P, P), f32), 1)], 1),
        "token_emb": a["tok_token_emb"],
        "weights": _np.concatenate([a["attn_W_qkv"], a["attn_W_proj"], a["ffn_Ws"]], 1),
        "rows": _np.concatenate([a["attn_b_qkv"], a["attn_b_proj"], a["ffn_bs"]])[None],
        "w1": w1,
        "w2": a["ffn_W2"].reshape(E, FC, P, D).transpose(2, 0, 1, 3),
        "b2": a["ffn_b2"][None],
    }
    nc = _bacc.Bacc("TRN2", target_bir_lowering=False, num_devices=1)
    args = []
    for name in arrays:
        arrays[name] = _np.ascontiguousarray(arrays[name])
        args.append(nc.dram_tensor(name, arrays[name].shape, mybir.dt.from_np(arrays[name].dtype),
                                   kind="ExternalInput").ap())
    args.append(nc.dram_tensor("out", (TOKENS, D), F32, kind="ExternalOutput").ap())
    build(nc, *args)
    r = _run(nc, [arrays], core_ids=[0])
    return r.results[0]["out"].reshape(*a["x"].shape, D)
```

```python
from contextlib import ExitStack

import concourse.bass as bass
import numpy as np
from concourse import mybir

ALU = mybir.AluOpType
ACT = mybir.ActivationFunctionType
AX = mybir.AxisListType
F32 = mybir.dt.float32
I32 = mybir.dt.int32
U32 = mybir.dt.uint32
BF16 = mybir.dt.bfloat16

P = 128
D = 128
H = 8
DH = D // H
HALF = D // 2
E = 8
F = 512
FC = F // P
TOKENS = 32 * 128
CAT, TIME0, NOTE0, VEL0, DUR0, VOCAB = 128, 128, 378, 410, 418, 668
TIME_STEPS = DUR_STEPS = 250
VEL_BINS = 32
ROWS = VOCAB + 1
TILES = -(-ROWS // P)
LAST = ROWS - (TILES - 1) * P
PAIRS = TILES // 2
NOTES_AND_VEL = VEL0 // P
VEL_AT = VEL0 % P
N_VEL = DUR0 - VEL0
EPS = 1e-5
SCALE = DH ** -0.5
BLOCKS = (ROWS - E) // P + E
JOBS = TOKENS // P
MM_JOBS = 14
DMA_JOBS = JOBS - MM_JOBS
MM_TOKENS = MM_JOBS * P
DMA_TOKENS = DMA_JOBS * P

TWO_PI_BELOW = 6.283185
ROUND = 1.5 * 2.0 ** 23
PHASE_ROWS = 7
DATA_ROWS = 4


def vocabulary_rows():
    v = np.arange(TILES * P)
    rows = np.zeros((PHASE_ROWS, TILES * P), np.float32)
    time = (v >= TIME0) & (v < NOTE0)
    note = (v >= NOTE0) & (v < VEL0)
    dur = (v >= DUR0) & (v < VOCAB)
    rows[0, time] = (v[time] - TIME0).astype(np.float32) / np.float32(TIME_STEPS)
    rows[1, time] = 1.0
    rows[2, dur] = (v[dur] - DUR0).astype(np.float32) / np.float32(DUR_STEPS)
    rows[3, dur] = 1.0
    rows[4, note] = (v[note] - NOTE0) // 12
    rows[5, note] = (v[note] - NOTE0) % 12
    rows[6, note] = 1.0
    return rows[:, P:]


def pitch_rows():
    i = np.arange(D // 4)
    rows = np.zeros((PHASE_ROWS - DATA_ROWS, D), np.float32)
    rows[0, 0::4] = rows[0, 1::4] = 2.0 ** -i / (2 * np.pi)
    rows[1, 2::4] = rows[1, 3::4] = (i + 1) / 12
    rows[2, 1::2] = 1 / 4
    return rows


def build(nc, x_dma, x_mm, phases, vel, vel_scale, consts, token_emb, weights, rows, w1, w2, b2, out):
    x2_sorted = nc.dram_tensor("x2_sorted", [ROWS + P - 1, D], F32)
    y_blocks = nc.dram_tensor("y_blocks", [BLOCKS * P, D], F32)
    table = nc.dram_tensor("table", [ROWS, D], F32)
    PAIR_ORDER = (0, 2, 1)
    with ExitStack() as ctx:
        def sb(name, shape, dt=F32):
            return ctx.enter_context(nc.sbuf_tensor(name, shape, dt))

        def sem(name):
            return ctx.enter_context(nc.semaphore(name))

        tok_in = sb("tok_in", [P, DMA_JOBS], I32)
        mm_in = sb("mm_in", [P, MM_TOKENS], I32)
        ph_in = sb("ph_in", [PHASE_ROWS, (TILES - 1) * P + HALF + D])
        row_basis = ph_in[:, 0:(TILES - 1) * P]
        lin_cols = ph_in[:, (TILES - 1) * P:(TILES - 1) * P + HALF]
        sin_cols = ph_in[:, (TILES - 1) * P + HALF:]
        vel_in = sb("vel_in", [HALF + 1, 2 * P + 2 + N_VEL])
        vel_hid, vel_w2 = vel_in[:, 0:P], vel_in[:, P:2 * P]
        vel_w1, vel_b1 = vel_in[0:HALF, 2 * P:2 * P + 1], vel_in[0:HALF, 2 * P + 1:2 * P + 2]
        vel_n = vel_in[0:HALF, 2 * P + 2:]
        vel_gb = sb("vel_gb", [P, 2, D])
        con = sb("con", [P, 2, P])
        ident, upper = con[:, 0, :], con[:, 1, :]
        w = sb("w", [P, 3 * D + D + E])
        w_v, w_proj, w_gate = w[:, 2 * D:3 * D], w[:, 3 * D:4 * D], w[:, 4 * D:]
        rw = sb("rw", [1, 3 * D + D + E])
        b_v, b_proj, b_gate = rw[:, 2 * D:3 * D], rw[:, 3 * D:4 * D], rw[:, 4 * D:]
        w1_sb = sb("w1_sb", [P, E, F + FC])
        w2_sb = sb("w2_sb", [P, E, FC, D])
        b2_sb = sb("b2_sb", [P, E, D])
        zeros = sb("zeros", [P, F], BF16)
        ones = sb("ones", [1, P])
        ones_bf = sb("ones_bf", [P, P], BF16)
        upper_bf = sb("upper_bf", [P, P], BF16)
        neg_half = sb("neg_half", [P, 2])
        tie_rank = sb("tie_rank", [P, E])
        expert_no = sb("expert_no", [1, E])
        block_no = sb("block_no", [1, BLOCKS])
        row_no = sb("row_no", [P, TILES])
        h = sb("h", [P, TILES, D])
        h_half = h.rearrange("p t (a n) -> p (t a) n", a=2)
        turns = sb("turns", [P, 7, HALF])
        frac = sb("frac", [P, 7, HALF])
        stats = sb("stats", [P, TILES + 1, 6])
        mv = sb("mv", [P, TILES + 1, 2])
        mv2 = sb("mv2", [P, TILES, 2])
        ve = sb("ve", [P, TILES + 1, 1])
        rstd = sb("rstd", [P, TILES + 1, 1])
        rstd2 = sb("rstd2", [P, TILES, 1])
        vn = sb("vn", [P, D])
        x1 = sb("x1", [P, TILES, D])
        x1T = sb("x1T", [P, TILES, P])
        hx = sb("hx", [P, TILES, D])
        wzv = sb("wzv", [P, 2, D])
        bzv = sb("bzv", [1, 2, D])
        zmax = sb("zmax", [P, TILES, H, 1])
        zs = sb("zs", [P, TILES, D])
        prob = sb("prob", [P, TILES, D])
        zsum = sb("zsum", [P, TILES, H, 1])
        zrec = sb("zrec", [P, TILES, H, 1])
        pv = sb("pv", [P, TILES, D])
        att = sb("att", [P, TILES, D])
        attT = sb("attT", [P, TILES, P])
        h2 = sb("h2", [P, TILES, D])
        x2 = sb("x2", [P, TILES, D])
        x2T = sb("x2T", [P, TILES, P])
        lmax = sb("lmax", [P, TILES, 1])
        lshift = sb("lshift", [P, TILES, E])
        lexp = sb("lexp", [P, TILES, E])
        lsum = sb("lsum", [P, TILES, 1])
        pmax = sb("pmax", [P, TILES, 1])
        best = sb("best", [P, TILES, E])
        omax = sb("omax", [P, TILES, 1])
        onehot = sb("onehot", [P, TILES, E], BF16)
        n_rows = sb("n_rows", [P, E])
        n_blocks = sb("n_blocks", [P, E])
        nil = sb("nil", [P, E])
        row_end = sb("row_end", [P, E])
        block_end = sb("block_end", [P, E])
        row_start = sb("row_start", [P, 1, E])
        block_start = sb("block_start", [P, 1, E])
        slot_start = sb("slot_start", [P, 1, E])
        place = sb("place", [P, 2, TILES, E])
        source = sb("source", [P, TILES, 1], U32)
        slot = sb("slot", [P, TILES, 1], U32)
        begun = sb("begun", [1, BLOCKS, E])
        ended = sb("ended", [1, BLOCKS, E])
        offset = sb("offset", [1, 1, E])
        sums = sb("sums", [1, 2, BLOCKS, 1])
        block_expert = sb("block_expert", [1, BLOCKS], I32)
        block_row = sb("block_row", [1, BLOCKS], I32)
        xb = sb("xb", [P, BLOCKS, D])
        xT = sb("xT", [P, 2, P])
        w1_now = sb("w1_now", [P, 3, F + FC])
        hid = sb("hid", [P, 2, FC, P])
        act_hid = sb("act_hid", [P, 2, FC, P])
        y = sb("y", [P, BLOCKS, D])
        y_row = sb("y_row", [P, TILES, D])
        tab = sb("tab", [P, TILES, D])
        tok = sb("tok", [P, DMA_JOBS], U32)
        mm_tok = sb("mm_tok", [P, MM_TOKENS])
        pick = sb("pick", [P, TILES, MM_TOKENS])
        got = sb("got", [P, DMA_JOBS, D])
        made = sb("made", [P, MM_JOBS, D])
        scratch = sb("scratch", [1, 2])

        ps = ctx.enter_context(nc.psum_tensor("ps", [P, 8, 512], F32))
        ps_lin = ps[:, 0, 0:5 * HALF].rearrange("p (t n) -> p t n", n=HALF)
        ps_sin = ps[:, 1, 0:7 * HALF].rearrange("p (t n) -> p t n", n=HALF)
        ps_vel = ps[:, 2, 0:P]
        ps_zv = [ps[:, g, :].rearrange("p (t k n) -> p t k n", t=2, k=2) for g in range(PAIRS)]
        ps_o = [ps[:, g, 0:2 * P].rearrange("p (t n) -> p t n", n=P) for g in range(PAIRS)]
        ps_turn = [ps[:, PAIRS + g, 0:2 * P].rearrange("p (t n) -> p t n", n=P) for g in range(PAIRS)]
        ps_gate = ps[:, 6, 0:TILES * E].rearrange("p (t e) -> p t e", e=E)
        ps_rank = ps[:, 6, 64:64 + (TILES + 1) * E].rearrange("p (t e) -> p t e", e=E)
        ps_idle = ps[:, 7, :]
        ps_xT = [ps[:, i, 0:P] for i in (0, 1)]
        ps_hid = [ps[:, i, :].rearrange("p (c n) -> p c n", n=P) for i in (2, 3)]
        ps_y = [ps[:, i, 0:P] for i in (4, 5)]

        phases_in, vel_loaded, scale_in, con_in, emb_in, w_in, rw_in, w1_in, w2_in, b2_in, tok_loaded, mm_loaded = (
            sem(n) for n in ("phases_in", "vel_loaded", "scale_in", "con_in", "emb_in", "w_in", "rw_in", "w1_in",
                             "w2_in", "b2_in", "tok_loaded", "mm_loaded"))
        zeros_set = sem("zeros_set")
        consts_set = sem("consts_set")
        cols_scaled = sem("cols_scaled")
        sin_phases = sem("sin_phases")
        lin_phases = sem("lin_phases")
        vel_hidden = sem("vel_hidden")
        vel_out = sem("vel_out")
        frac_done = sem("frac_done")
        sines_done = sem("sines_done")
        dve_seq = sem("dve_seq")
        pool_seq = sem("pool_seq")
        var_done = sem("var_done")
        rstd_done = sem("rstd_done")
        x1_done = sem("x1_done")
        x1T_ps = sem("x1T_ps")
        x1T_done = sem("x1T_done")
        wzv_done = sem("wzv_done")
        hx_done = sem("hx_done")
        zv_done = sem("zv_done")
        zs_done = sem("zs_done")
        exp_done = sem("exp_done")
        att_done = sem("att_done")
        attT_ps = sem("attT_ps")
        attT_done = sem("attT_done")
        o_done = sem("o_done")
        x2_done = sem("x2_done")
        x2T_ps = sem("x2T_ps")
        x2T_done = sem("x2T_done")
        gate_done = sem("gate_done")
        lshift_done = sem("lshift_done")
        lexp_done = sem("lexp_done")
        onehot_done = sem("onehot_done")
        upper_done = sem("upper_done")
        rank_done = sem("rank_done")
        source_done = sem("source_done")
        slot_done = sem("slot_done")
        blocks_done = sem("blocks_done")
        slack_out = sem("slack_out")
        rows_sorted = sem("rows_sorted")
        block_in = [sem(f"block_in{b}") for b in range(BLOCKS)]
        xT_ps = sem("xT_ps")
        xT_done = sem("xT_done")
        w1_staged = sem("w1_staged")
        up_done = sem("up_done")
        biased = sem("biased")
        gelu_done = sem("gelu_done")
        down_done = sem("down_done")
        y_done = sem("y_done")
        y_out = sem("y_out")
        y_back = [sem(f"y_back{t}") for t in range(TILES)]
        tab_done = sem("tab_done")
        table_out = sem("table_out")
        tok_done = sem("tok_done")
        pick_done = sem("pick_done")
        picked = sem("picked")
        made_done = sem("made_done")
        DMA_PARTS = ((0, 6), (6, 12), (12, DMA_JOBS))
        rows_got = [sem(f"rows_got{i}") for i in range(len(DMA_PARTS))]
        out_done = sem("out_done")
        MM_BANK = 4
        MM_BANKS = -(-MM_JOBS // MM_BANK)

        ctx.enter_context(nc.allow_low_precision("sums of small whole numbers are exact"))

        def last_rows(t):
            return P if t < TILES - 1 else LAST

        block = ctx.enter_context(nc.Block())

        @block.sync
        def _(sp):
            sp.dma_start(ph_in[:, :], phases[:, :]).then_inc(phases_in, 16)
            sp.dma_start(con[:, :, :], consts[:, :, :]).then_inc(con_in, 16)
            sp.dma_start(w[:, :], weights[:, :]).then_inc(w_in, 16)
            sp.dma_start(rw[:, :], rows[:, :]).then_inc(rw_in, 16)
            sp.dma_start(w1_sb[:, :, :], w1[:, :, :]).then_inc(w1_in, 16)
            sp.dma_start(w2_sb[:, :, :, :], w2[:, :, :, :]).then_inc(w2_in, 16)
            sp.dma_start(b2_sb[:, :, :], b2.broadcast_to([P, E, D])).then_inc(b2_in, 16)
            sp.dma_start(mm_in[:, :], x_mm.broadcast_to([P, MM_TOKENS])).then_inc(mm_loaded, 16)
            sp.wait_ge(blocks_done, 1)
            sp.wait_ge(slack_out, 16)
            sp.wait_ge(rows_sorted, TILES * 16)
            for b in range(BLOCKS):
                row = sp.value_load(block_row[0:1, b:b + 1], min_val=0, max_val=ROWS - 1)
                sp.dma_start(xb[:, b, :], x2_sorted.ap()[bass.ds(row, P), :]).then_inc(block_in[b], 16)
            for b in range(BLOCKS):
                sp.wait_ge(y_done, b + 1)
                sp.dma_start(y_blocks.ap()[b * P:(b + 1) * P, :], y[:, b, :]).then_inc(y_out, 16)
            sp.wait_ge(tab_done, TILES)
            full = (TILES - 1) * P
            sp.dma_start(table.ap()[0:full, :].rearrange("(t p) n -> p t n", p=P),
                         tab[:, 0:TILES - 1, :]).then_inc(table_out, 16)
            sp.dma_start(table.ap()[full:, :], tab[0:LAST, TILES - 1, :]).then_inc(table_out, 16)
            for c, (a, b) in enumerate(DMA_PARTS):
                sp.wait_ge(rows_got[c], (b - a) * 16)
                sp.dma_start(out[0:DMA_TOKENS, :].rearrange("(p j) n -> p j n", p=P)[:, a:b, :],
                             got[:, a:b, :]).then_inc(out_done, 16)
            sp.wait_ge(out_done, 16 * (len(DMA_PARTS) + MM_BANKS))

        @block.gpsimd
        def _(pool):
            seq = [0]

            def then(ins):
                seq[0] += 1
                ins.then_inc(pool_seq, 1)
                pool.wait_ge(pool_seq, seq[0])

            pool.memset(neg_half[:, :], -0.5)
            pool.memset(ones[:, :], 1.0)
            pool.memset(ones_bf[:, :], 1.0)
            pool.memset(nil[:, :], 0.0)
            pool.memset(onehot[:, TILES - 1, :], 0.0)
            pool.iota(tie_rank[:, :], [[-1, E]], base=E, channel_multiplier=0, allow_small_or_imprecise_dtypes=True)
            pool.iota(expert_no[:, :], [[1, E]], base=0, channel_multiplier=0, allow_small_or_imprecise_dtypes=True)
            pool.iota(block_no[:, :], [[1, BLOCKS]], base=0, channel_multiplier=0,
                      allow_small_or_imprecise_dtypes=True)
            pool.iota(row_no[:, :], [[P, TILES]], base=0, channel_multiplier=1,
                      allow_small_or_imprecise_dtypes=True).then_inc(consts_set, 1)
            pool.wait_ge(consts_set, 1)

            n_var = [0]

            def inverse_root(n, at, m, r):
                n_var[0] += 1
                pool.wait_ge(var_done, n_var[0])
                k = at.stop - at.start
                then(pool.tensor_scalar(ve[0:n, at, 0], m[0:n, at, 1], EPS, 0.0, ALU.add, ALU.add))
                pool.tensor_tensor(r[0:n, at, 0], ve[0:n, at, 0], neg_half[0:n, 0:k], ALU.pow).then_inc(rstd_done, 1)

            def residual(i, g):
                a = slice(2 * g, 2 * g + 2)
                pool.wait_ge(x1_done, i + 1)
                pool.tensor_tensor(hx[:, a, :], h[:, a, :], x1[:, a, :], ALU.add).then_inc(hx_done, 1)

            def pair_root(g, m, r):
                inverse_root(P, slice(2 * g, 2 * g + 2), m, r)

            inverse_root(HALF, slice(TILES, TILES + 1), mv, rstd)
            pair_root(PAIR_ORDER[0], mv, rstd)
            pair_root(PAIR_ORDER[1], mv, rstd)
            residual(0, PAIR_ORDER[0])
            pair_root(PAIR_ORDER[2], mv, rstd)
            residual(1, PAIR_ORDER[1])
            residual(2, PAIR_ORDER[2])
            for g in PAIR_ORDER:
                pair_root(g, mv2, rstd2)
            pool.wait_ge(source_done, 1)
            for t in range(TILES):
                n = last_rows(t)
                pool.indirect_dma_start(
                    out=x2_sorted.ap()[:, :], out_offset=bass.IndirectOffsetOnAxis(ap=source[0:n, t, :], axis=0),
                    in_=x2[0:n, t, :], in_offset=None).then_inc(rows_sorted, 16)
            pool.wait_ge(slot_done, 1)
            pool.wait_ge(y_out, BLOCKS * 16)
            for t in range(TILES):
                n = last_rows(t)
                pool.indirect_dma_start(
                    out=y_row[0:n, t, :], out_offset=None, in_=y_blocks.ap()[:, :],
                    in_offset=bass.IndirectOffsetOnAxis(ap=slot[0:n, t, :], axis=0)).then_inc(y_back[t], 16)
            pool.wait_ge(tok_done, 1)
            pool.wait_ge(table_out, 2 * 16)
            for c, (a, b) in enumerate(DMA_PARTS):
                for j in range(a, b):
                    pool.indirect_dma_start(
                        out=got[:, j, :], out_offset=None, in_=table.ap()[:, :],
                        in_offset=bass.IndirectOffsetOnAxis(ap=tok[:, j:j + 1], axis=0)).then_inc(rows_got[c], 16)

        @block.scalar
        def _(act):
            act.dma_start(vel_in[:, :], vel[:, :]).then_inc(vel_loaded, 16)
            act.dma_start(h[:, 0, :], token_emb[:, :]).then_inc(emb_in, 16)
            act.dma_start(vel_gb[:, :, :], vel_scale[:, :, :]).then_inc(scale_in, 16)
            act.dma_start(tok_in[:, :], x_dma[:, :]).then_inc(tok_loaded, 16)
            act.wait_ge(zeros_set, 1)
            act.dma_start(x2_sorted.ap()[ROWS:, :], zeros[0:P - 1, 0:2 * D].bitcast(F32)).then_inc(slack_out, 16)
            act.wait_ge(vel_loaded, 16)
            act.activation(vel_hid[0:HALF, VEL_AT:VEL_AT + N_VEL], vel_n, ACT.Gelu,
                           bias=vel_b1, scale=vel_w1).then_inc(vel_hidden, 1)
            act.activation(scratch[:, 0:1], zeros[0:1, 0:1], ACT.Sin)
            act.wait_ge(frac_done, 1)
            act.activation(h_half[:, 3:8, :], frac[:, 0:5, :], ACT.Sin, scale=TWO_PI_BELOW)
            act.activation(h_half[:, 9:12:2, :], frac[:, 5:7, :], ACT.Sin, scale=TWO_PI_BELOW)
            act.wait_ge(lin_phases, 1)
            act.activation(h_half[:, 2, :], ps_lin[:, 0, :], ACT.Copy)
            act.activation(h_half[:, 8:11:2, :], ps_lin[:, 3:5, :], ACT.Copy).then_inc(sines_done, 1)
            act.activation(scratch[:, 1:2], zeros[0:1, 0:1], ACT.Exp)

            def x1T_copy(i, g):
                act.wait_ge(x1T_ps, i + 1)
                act.activation(x1T[:, 2 * g:2 * g + 2, :], ps_turn[g], ACT.Copy).then_inc(x1T_done, 1)

            def exps(i, g):
                act.wait_ge(zs_done, i + 1)
                act.activation(prob[:, 2 * g:2 * g + 2, :], zs[:, 2 * g:2 * g + 2, :], ACT.Exp,
                               scale=SCALE).then_inc(exp_done, 1)

            def attT_copy(i, g):
                act.wait_ge(attT_ps, i + 1)
                act.activation(attT[:, 2 * g:2 * g + 2, :], ps_turn[g], ACT.Copy).then_inc(attT_done, 1)

            def x2T_copy(i, g):
                act.wait_ge(x2T_ps, i + 1)
                act.activation(x2T[:, 2 * g:2 * g + 2, :], ps_turn[g], ACT.Copy).then_inc(x2T_done, 1)

            for step, i in ((x1T_copy, 0), (x1T_copy, 1), (exps, 0), (x1T_copy, 2), (exps, 1), (attT_copy, 0),
                            (exps, 2), (attT_copy, 1), (attT_copy, 2), (x2T_copy, 0), (x2T_copy, 1), (x2T_copy, 2)):
                step(i, PAIR_ORDER[i])
            act.wait_ge(lshift_done, 1)
            act.activation(lexp[:, :, :], lshift[:, :, :], ACT.Exp).then_inc(lexp_done, 1)

            def xT_copy(b):
                act.wait_ge(xT_ps, b + 1)
                if b >= 2:
                    act.wait_ge(up_done, b - 1)
                act.activation(xT[:, b % 2, :], ps_xT[b % 2], ACT.Copy).then_inc(xT_done, 1)

            def gelu(b):
                act.wait_ge(biased, b + 1)
                if b >= 2:
                    act.wait_ge(down_done, b - 1)
                act.activation(act_hid[:, b % 2, :, :], hid[:, b % 2, :, :], ACT.Gelu).then_inc(gelu_done, 1)

            xT_copy(0)
            for b in range(BLOCKS):
                if b + 1 < BLOCKS:
                    xT_copy(b + 1)
                gelu(b)
            for c in range(MM_BANKS):
                a, b = c * MM_BANK, min(c * MM_BANK + MM_BANK, MM_JOBS)
                act.wait_ge(picked, c + 1)
                act.activation(made[:, a:b, :], ps[:, c, 0:(b - a) * D].rearrange("p (j n) -> p j n", n=D),
                               ACT.Copy).then_inc(made_done, 1)
                act.wait_ge(made_done, c + 1)
                act.dma_start(out[DMA_TOKENS:, :].rearrange("(p j) n -> p j n", p=P)[:, a:b, :],
                              made[:, a:b, :]).then_inc(out_done, 16)

        @block.tensor
        def _(pe):
            def keep_warm(n):
                for _ in range(n):
                    pe.matmul(ps_idle, zeros[:, 0:P], zeros[:, :], start=True, stop=True)

            pe.wait_ge(zeros_set, 1)
            keep_warm(6)
            pe.wait_ge(phases_in, 16)
            pe.wait_ge(cols_scaled, 1)
            for at, t, cols in ((0, 0, slice(HALF, D)), (1, 1, slice(0, D)), (3, 2, slice(0, D)),
                                (5, 3, slice(HALF, D)), (6, 4, slice(HALF, D))):
                n = cols.stop - cols.start
                mm = pe.matmul(ps[:, 1, at * HALF:at * HALF + n], row_basis[:, t * P:(t + 1) * P],
                               sin_cols[:, cols], start=True, stop=True)
            mm.then_inc(sin_phases, 1)
            for t in range(TILES - 1):
                mm = pe.matmul(ps_lin[:, t, :], row_basis[:, t * P:(t + 1) * P], lin_cols, start=True, stop=True)
            mm.then_inc(lin_phases, 1)
            pe.wait_ge(vel_hidden, 1)
            pe.matmul(ps_vel, vel_hid, vel_w2, start=True, stop=True).then_inc(vel_out, 1)
            pe.wait_ge(rw_in, 16)
            pe.wait_ge(consts_set, 1)
            pe.matmul(ps_gate, ones[:, :], b_gate.rearrange("p (t e) -> p t e", t=1).broadcast_to([1, TILES, E]),
                      start=True, stop=False, skip_group_check=True)

            def x1_turn(i, g):
                if i == 0:
                    pe.wait_ge(con_in, 16)
                    keep_warm(10)
                pe.wait_ge(x1_done, i + 1)
                for t in range(2):
                    mm = pe.transpose(ps_turn[g][:, t, :], x1[:, 2 * g + t, :], ident)
                mm.then_inc(x1T_ps, 1)
                if i == 0:
                    pe.wait_ge(wzv_done, 1)
                bias = bzv.rearrange("p k n -> p (k n)").rearrange("p (t m) -> p t m", t=1)
                pe.matmul(ps_zv[g].rearrange("p t k n -> p t (k n)"), ones[:, :], bias.broadcast_to([1, 2, 2 * D]),
                          start=True, stop=False, skip_group_check=True)

            def scores(i, g):
                pe.wait_ge(x1T_done, i + 1)
                for t in range(2):
                    mm = pe.matmul(ps_zv[g][:, t, :, :].rearrange("p k n -> p (k n)"), x1T[:, 2 * g + t, :],
                                   wzv.rearrange("p k n -> p (k n)"), start=False, stop=True, skip_group_check=True)
                mm.then_inc(zv_done, 1)

            def att_turn(i, g):
                keep_warm(2)
                pe.wait_ge(att_done, i + 1)
                for t in range(2):
                    mm = pe.transpose(ps_turn[g][:, t, :], att[:, 2 * g + t, :], ident)
                mm.then_inc(attT_ps, 1)
                pe.matmul(ps_o[g], ones[:, :], b_proj.rearrange("p (t n) -> p t n", t=1).broadcast_to([1, 2, D]),
                          start=True, stop=False, skip_group_check=True)

            def project(i, g):
                pe.wait_ge(attT_done, i + 1)
                for t in range(2):
                    mm = pe.matmul(ps_o[g][:, t, :], attT[:, 2 * g + t, :], w_proj, start=False, stop=True,
                                   skip_group_check=True)
                mm.then_inc(o_done, 1)

            def x2_turn(i, g):
                keep_warm(2)
                pe.wait_ge(x2_done, i + 1)
                for t in range(2):
                    mm = pe.transpose(ps_turn[g][:, t, :], x2[:, 2 * g + t, :], ident)
                mm.then_inc(x2T_ps, 1)

            def gate(i, g):
                pe.wait_ge(x2T_done, i + 1)
                for t in range(2 * g, 2 * g + 2):
                    mm = pe.matmul(ps_gate[:, t, :], x2T[:, t, :], w_gate, start=False, stop=True,
                                   skip_group_check=True)
                if i == PAIRS - 1:
                    mm.then_inc(gate_done, 1)

            for step, i in ((x1_turn, 0), (x1_turn, 1), (scores, 0), (x1_turn, 2), (scores, 1), (scores, 2),
                            (att_turn, 0), (project, 0), (att_turn, 1), (project, 1), (att_turn, 2), (project, 2),
                            (x2_turn, 0), (gate, 0), (x2_turn, 1), (gate, 1), (x2_turn, 2), (gate, 2)):
                step(i, PAIR_ORDER[i])
            keep_warm(6)
            pe.wait_ge(onehot_done, 1)
            pe.wait_ge(upper_done, 1)
            pe.matmul(ps_rank[:, 0:TILES, :], upper_bf[:, :], onehot[:, :, :], start=True, stop=False,
                      skip_group_check=True)
            for s in range(1, TILES + 1):
                mm = pe.matmul(ps_rank[:, s:TILES + 1, :], ones_bf[:, :], onehot[:, 0:TILES + 1 - s, :],
                               start=False, stop=(s == TILES), skip_group_check=True)
            mm.then_inc(rank_done, 1)
            pe.wait_ge(blocks_done, 1)
            pe.wait_ge(w2_in, 16)

            def turn(b):
                pe.wait_ge(block_in[b], 16)
                if b >= 2:
                    pe.wait_ge(xT_done, b - 1)
                pe.transpose(ps_xT[b % 2], xb[:, b, :], ident).then_inc(xT_ps, 1)

            def up(b):
                pe.wait_ge(w1_staged, b + 1)
                pe.wait_ge(xT_done, b + 1)
                if b >= 2:
                    pe.wait_ge(biased, b - 1)
                for c in range(FC):
                    mm = pe.matmul(ps_hid[b % 2][:, c, :], w1_now[:, b % 3, c * P:(c + 1) * P], xT[:, b % 2, :],
                                   start=True, stop=True)
                mm.then_inc(up_done, 1)

            def down(b):
                e = pe.value_load(block_expert[0:1, b:b + 1], min_val=0, max_val=E - 1)
                pe.wait_ge(gelu_done, b + 1)
                if b >= 2:
                    pe.wait_ge(y_done, b - 1)
                for c in range(FC):
                    mm = pe.matmul(ps_y[b % 2], act_hid[:, b % 2, c, :], w2_sb[:, bass.ds(e, 1), c, :],
                                   start=(c == 0), stop=(c == FC - 1))
                mm.then_inc(down_done, 1)

            turn(0)
            up(0)
            turn(1)
            for b in range(BLOCKS):
                if b + 1 < BLOCKS:
                    up(b + 1)
                if b + 2 < BLOCKS:
                    turn(b + 2)
                down(b)
            keep_warm(16)
            for c in range(MM_BANKS):
                for j in range(c * MM_BANK, min(c * MM_BANK + MM_BANK, MM_JOBS)):
                    for t in range(TILES):
                        if j == 0:
                            pe.wait_ge(pick_done, t + 1)
                            pe.wait_ge(tab_done, t + 1)
                        n = last_rows(t)
                        mm = pe.matmul(ps[:, c, (j % MM_BANK) * D:(j % MM_BANK + 1) * D],
                                       pick[0:n, t, j * P:(j + 1) * P], tab[0:n, t, :],
                                       start=(t == 0), stop=(t == TILES - 1))
                mm.then_inc(picked, 1)

        @block.vector
        def _(dve):
            seq = [0]

            def then(ins):
                seq[0] += 1
                ins.then_inc(dve_seq, 1)
                dve.wait_ge(dve_seq, seq[0])

            n_root = [0]

            def root_ready():
                n_root[0] += 1
                dve.wait_ge(rstd_done, n_root[0])

            dve.memset(zeros[:, :].bitcast(U32), 0).then_inc(zeros_set, 1)
            dve.wait_ge(phases_in, 16)
            dve.tensor_scalar(sin_cols[0:DATA_ROWS, :], sin_cols[0:DATA_ROWS, :], float(1 / (2 * np.pi)), None,
                              ALU.mult).then_inc(cols_scaled, 1)
            dve.wait_ge(sin_phases, 1)
            then(dve.tensor_scalar(turns[:, :, :], ps_sin, ROUND, ROUND, ALU.add, ALU.subtract))
            dve.tensor_tensor(frac[:, :, :], ps_sin, turns[:, :, :], ALU.subtract).then_inc(frac_done, 1)
            n = HALF
            dve.wait_ge(vel_out, 1)
            then(dve.bn_stats(stats[0:n, TILES, :], ps_vel[0:n, :]))
            dve.bn_aggr(mv[0:n, TILES, :], stats[0:n, TILES, :]).then_inc(var_done, 1)
            dve.wait_ge(con_in, 16)
            dve.tensor_copy(upper_bf[:, :], upper).then_inc(upper_done, 1)
            dve.wait_ge(tok_loaded, 16)
            dve.tensor_scalar(tok[:, :], tok_in[:, :], float(VOCAB), 0.0, ALU.min, ALU.max).then_inc(tok_done, 1)
            root_ready()
            then(dve.tensor_scalar(vn[0:n, :], ps_vel[0:n, :], mv[0:n, TILES, 0:1], rstd[0:n, TILES, :],
                                   ALU.subtract, ALU.mult))
            dve.wait_ge(scale_in, 16)
            then(dve.tensor_tensor(vn[0:n, :], vn[0:n, :], vel_gb[0:n, 0, :], ALU.mult))
            then(dve.tensor_tensor(vn[0:n, :], vn[0:n, :], vel_gb[0:n, 1, :], ALU.add))

            def stat(src, m, g):
                for t in (2 * g, 2 * g + 1):
                    ins = dve.bn_stats(stats[:, t, :], src[:, t, :])
                then(ins)
                for t in (2 * g, 2 * g + 1):
                    ins = dve.bn_aggr(m[:, t, :], stats[:, t, :])
                ins.then_inc(var_done, 1)

            def norm(src, m, r, dst, done, g):
                root_ready()
                for t in (2 * g, 2 * g + 1):
                    ins = dve.tensor_scalar(dst[:, t, :], src[:, t, :], m[:, t, 0:1], r[:, t, :],
                                            ALU.subtract, ALU.mult)
                ins.then_inc(done, 1)

            def stat1(i, g):
                stat(h, mv, g)

            def norm1(i, g):
                norm(h, mv, rstd, x1, x1_done, g)

            def heads(ap):
                return ap.rearrange("p t (h d) -> p t h d", d=DH)

            def wide(ap):
                return ap.broadcast_to([P, 2, H, DH])

            def shift(i, g):
                a = slice(2 * g, 2 * g + 2)
                dve.wait_ge(zv_done, i + 1)
                z = heads(ps_zv[g][:, :, 0, :])
                then(dve.tensor_reduce(zmax[:, a, :, :], z, AX.X, ALU.max))
                dve.tensor_tensor(heads(zs[:, a, :]), z, wide(zmax[:, a, :, :]), ALU.subtract).then_inc(zs_done, 1)

            def weigh(i, g):
                a = slice(2 * g, 2 * g + 2)
                dve.wait_ge(exp_done, i + 1)
                then(dve.tensor_reduce(zsum[:, a, :, :], heads(prob[:, a, :]), AX.X, ALU.add))
                dve.tensor_tensor(pv[:, a, :], prob[:, a, :], ps_zv[g][:, :, 1, :], ALU.mult)
                then(dve.reciprocal(zrec[:, a, :, :], zsum[:, a, :, :]))
                dve.tensor_tensor(heads(att[:, a, :]), heads(pv[:, a, :]), wide(zrec[:, a, :, :]),
                                  ALU.mult).then_inc(att_done, 1)

            def stat2(i, g):
                dve.wait_ge(o_done, i + 1)
                dve.wait_ge(hx_done, i + 1)
                a = slice(2 * g, 2 * g + 2)
                then(dve.tensor_tensor(h2[:, a, :], hx[:, a, :], ps_o[g], ALU.add))
                stat(h2, mv2, g)

            def norm2(i, g):
                norm(h2, mv2, rstd2, x2, x2_done, g)

            dve.wait_ge(w_in, 16)
            dve.wait_ge(rw_in, 16)
            dve.tensor_tensor(wzv[:, 0, :], w[:, 0:D], w[:, D:2 * D], ALU.subtract)
            dve.tensor_copy(wzv[:, 1, :], w_v)
            dve.tensor_tensor(bzv[:, 0, :], rw[:, 0:D], rw[:, D:2 * D], ALU.subtract)
            dve.tensor_copy(bzv[:, 1, :], b_v).then_inc(wzv_done, 1)
            dve.wait_ge(sines_done, 1)
            dve.wait_ge(emb_in, 16)
            stat1(0, PAIR_ORDER[0])
            then(dve.tensor_tensor(h_half[:, 4:7:2, :], h_half[:, 4:7:2, :], ps_lin[:, 1:3, :], ALU.add))
            stat1(1, PAIR_ORDER[1])
            norm1(0, PAIR_ORDER[0])
            t = NOTES_AND_VEL
            then(dve.tensor_tensor(h[0:n, t, :], h[0:n, t, :], vn[0:n, :], ALU.add))
            for step, i in ((stat1, 2), (norm1, 1), (norm1, 2), (shift, 0), (shift, 1), (weigh, 0), (shift, 2),
                            (weigh, 1), (stat2, 0), (weigh, 2), (norm2, 0), (stat2, 1), (stat2, 2), (norm2, 1),
                            (norm2, 2)):
                step(i, PAIR_ORDER[i])
            dve.wait_ge(gate_done, 1)
            then(dve.tensor_reduce(lmax[:, :, :], ps_gate, AX.X, ALU.max))
            wide_max = lmax[:, :, :].broadcast_to([P, TILES, E])
            then(dve.tensor_tensor(best[:, :, :], ps_gate, wide_max, ALU.is_equal))
            dve.tensor_tensor(lshift[:, :, :], ps_gate, wide_max, ALU.subtract).then_inc(lshift_done, 1)
            dve.wait_ge(consts_set, 1)
            then(dve.tensor_tensor(best[:, :, :], best[:, :, :],
                                   tie_rank.rearrange("p (a e) -> p a e", a=1).broadcast_to([P, TILES, E]), ALU.mult))
            then(dve.tensor_reduce(omax[:, :, :], best[:, :, :], AX.X, ALU.max))
            for a, b, n in ((0, TILES - 1, P), (TILES - 1, TILES, LAST)):
                ins = dve.tensor_tensor(onehot[0:n, a:b, :], best[0:n, a:b, :],
                                        omax[0:n, a:b, :].broadcast_to([n, b - a, E]), ALU.is_equal)
            ins.then_inc(onehot_done, 1)
            dve.wait_ge(lexp_done, 1)
            then(dve.tensor_reduce(lsum[:, :, :], lexp[:, :, :], AX.X, ALU.add))
            dve.reciprocal(pmax[:, :, :], lsum[:, :, :])
            dve.wait_ge(rank_done, 1)
            then(dve.tensor_copy(n_rows[:, :], ps_rank[:, TILES, :]))
            then(dve.tensor_tensor_scan(row_end[:, :], n_rows[:, :], nil[:, :], 0.0, ALU.add, ALU.add))
            then(dve.tensor_tensor(row_start[:, 0, :], row_end[:, :], n_rows[:, :], ALU.subtract))

            def places(k, start, dst, done):
                ranks = ps_rank[:, 0:TILES, :]
                then(dve.tensor_tensor(place[:, k, :, :], ranks, start[:, :, :].broadcast_to([P, TILES, E]), ALU.add))
                then(dve.tensor_tensor(place[:, k, :, :], place[:, k, :, :], onehot[:, :, :], ALU.mult))
                dve.tensor_reduce(dst[:, :, :], place[:, k, :, :], AX.X, ALU.add).then_inc(done, 1)

            places(0, row_start, source, source_done)
            then(dve.tensor_scalar(n_blocks[:, :], n_rows[:, :], (P - 1) / 2, 1 / P, ALU.add, ALU.mult))
            then(dve.tensor_scalar(n_blocks[:, :], n_blocks[:, :], ROUND, ROUND, ALU.add, ALU.subtract))
            then(dve.tensor_tensor_scan(block_end[:, :], n_blocks[:, :], nil[:, :], 0.0, ALU.add, ALU.add))
            then(dve.tensor_tensor(block_start[:, 0, :], block_end[:, :], n_blocks[:, :], ALU.subtract))
            then(dve.tensor_scalar(slot_start[:, 0, :], block_start[:, 0, :], float(P), None, ALU.mult))
            grid = [1, BLOCKS, E]
            number = block_no.rearrange("p (b e) -> p b e", e=1)
            dve.tensor_tensor(begun[:, :, :], number.broadcast_to(grid), block_start[0:1, :, :].broadcast_to(grid),
                              ALU.is_ge)
            dve.tensor_tensor(ended[:, :, :], number.broadcast_to(grid),
                              block_end[0:1, :].rearrange("p (b e) -> p b e", b=1).broadcast_to(grid), ALU.is_ge)
            then(dve.tensor_tensor(offset[:, :, :], row_start[0:1, :, :], slot_start[0:1, :, :], ALU.subtract))
            then(dve.tensor_tensor(begun[:, :, :], begun[:, :, :], ended[:, :, :], ALU.subtract))
            dve.tensor_tensor(ended[:, :, :], begun[:, :, :],
                              expert_no.rearrange("p (b e) -> p b e", b=1).broadcast_to(grid), ALU.mult)
            then(dve.tensor_tensor(begun[:, :, :], begun[:, :, :], offset[:, :, :].broadcast_to(grid), ALU.mult))
            dve.tensor_reduce(block_expert.rearrange("p (b e) -> p b e", e=1), ended[:, :, :], AX.X, ALU.add)
            then(dve.tensor_reduce(sums[:, 0, :, :], begun[:, :, :], AX.X, ALU.add))
            then(dve.scalar_tensor_tensor(sums[:, 1, :, :], number, float(P), sums[:, 0, :, :], ALU.mult, ALU.add))
            dve.tensor_scalar(block_row[:, :], sums[:, 1, :, 0], float(ROWS - 1), None, ALU.min).then_inc(blocks_done, 1)
            places(1, slot_start, slot, slot_done)
            dve.wait_ge(blocks_done, 1)
            dve.wait_ge(w1_in, 16)
            dve.wait_ge(b2_in, 16)

            def stage(b):
                e = dve.value_load(block_expert[0:1, b:b + 1], min_val=0, max_val=E - 1)
                if b >= 3:
                    dve.wait_ge(up_done, b - 2)
                    dve.wait_ge(biased, b - 2)
                dve.tensor_copy(w1_now[:, b % 3, :], w1_sb[:, bass.ds(e, 1), :].rearrange("p a n -> p (a n)")
                                ).then_inc(w1_staged, 1)
                return e

            def bias(b):
                dve.wait_ge(up_done, b + 1)
                if b >= 2:
                    dve.wait_ge(gelu_done, b - 1)
                b1 = w1_now[:, b % 3, F:].rearrange("p (c n) -> p c n", n=1).broadcast_to([P, FC, P])
                dve.tensor_tensor(hid[:, b % 2, :, :], ps_hid[b % 2], b1, ALU.add).then_inc(biased, 1)

            def finish(b, e):
                dve.wait_ge(down_done, b + 1)
                dve.tensor_tensor(y[:, b, :], ps_y[b % 2], b2_sb[:, bass.ds(e, 1), :].rearrange("p a n -> p (a n)"),
                                  ALU.add).then_inc(y_done, 1)

            experts = [stage(0), stage(1)]
            dve.wait_ge(mm_loaded, 16)
            then(dve.tensor_scalar(mm_tok[:, :], mm_in[:, :], float(VOCAB), 0.0, ALU.min, ALU.max))
            for t in range(TILES):
                dve.tensor_scalar(pick[:, t, :], mm_tok[:, :], row_no[:, t:t + 1], None, ALU.is_equal
                                  ).then_inc(pick_done, 1)
            for b in range(BLOCKS):
                bias(b)
                if b + 2 < BLOCKS:
                    experts.append(stage(b + 2))
                if b >= 1:
                    finish(b - 1, experts[b - 1])
            finish(BLOCKS - 1, experts[-1])
            for t in range(TILES):
                n = last_rows(t)
                dve.wait_ge(y_back[t], 16)
                dve.scalar_tensor_tensor(tab[0:n, t, :], y_row[0:n, t, :], pmax[0:n, t, :], h2[0:n, t, :],
                                         ALU.mult, ALU.add).then_inc(tab_done, 1)


def kernel(**inputs):
    import numpy as _np
    import concourse.bacc as _bacc
    from concourse.bass_utils import run_bass_kernel_spmd as _run

    a = {k.removeprefix("L0_"): _np.asarray(v) for k, v in inputs.items()}
    f32 = _np.float32
    x = a["x"].reshape(-1)

    sines = _np.zeros((PHASE_ROWS, HALF + D), f32)
    for k, name in enumerate(("time_lin_w", "time_lin_b", "dur_lin_w", "dur_lin_b")):
        sines[k, 0:HALF] = a["tok_" + name]
    for k, name in enumerate(("time_w", "time_b", "dur_w", "dur_b")):
        sines[k, HALF + HALF:] = a["tok_" + name]
    sines[4:, HALF:] = pitch_rows()

    vel = _np.zeros((HALF + 1, 2 * P + 2 + N_VEL), f32)
    vel[HALF, VEL_AT:VEL_AT + N_VEL] = 1.0
    vel[0:HALF, P:2 * P] = a["tok_vel_w2"].T
    vel[HALF, P:2 * P] = a["tok_vel_b2"]
    vel[0:HALF, 2 * P] = a["tok_vel_w1"]
    vel[0:HALF, 2 * P + 1] = a["tok_vel_b1"]
    vel[:, 2 * P + 2:] = _np.arange(N_VEL, dtype=f32) / f32(VEL_BINS)
    vel_scale = _np.zeros((P, 2, D), f32)
    vel_scale[VEL_AT:VEL_AT + N_VEL, 0] = a["tok_vel_ln_g"]
    vel_scale[VEL_AT:VEL_AT + N_VEL, 1] = a["tok_vel_ln_b"]

    w1 = _np.zeros((P, E, F + FC), f32)
    w1[:, :, 0:F] = a["ffn_W1"].transpose(1, 0, 2)
    w1[:, :, F:] = a["ffn_b1"].reshape(E, FC, P).transpose(2, 0, 1)
    arrays = {
        "x_dma": x[:DMA_TOKENS].reshape(P, DMA_JOBS),
        "x_mm": x[DMA_TOKENS:].reshape(P, MM_JOBS).T.reshape(1, MM_TOKENS),
        "phases": _np.concatenate([vocabulary_rows(), sines], 1),
        "vel": vel,
        "vel_scale": vel_scale,
        "consts": _np.stack([_np.eye(P, dtype=f32), _np.triu(_np.ones((P, P), f32), 1)], 1),
        "token_emb": a["tok_token_emb"],
        "weights": _np.concatenate([a["attn_W_qkv"], a["attn_W_proj"], a["ffn_Ws"]], 1),
        "rows": _np.concatenate([a["attn_b_qkv"], a["attn_b_proj"], a["ffn_bs"]])[None],
        "w1": w1,
        "w2": a["ffn_W2"].reshape(E, FC, P, D).transpose(2, 0, 1, 3),
        "b2": a["ffn_b2"][None],
    }
    nc = _bacc.Bacc("TRN2", target_bir_lowering=False, num_devices=1)
    args = []
    for name in arrays:
        arrays[name] = _np.ascontiguousarray(arrays[name])
        args.append(nc.dram_tensor(name, arrays[name].shape, mybir.dt.from_np(arrays[name].dtype),
                                   kind="ExternalInput").ap())
    args.append(nc.dram_tensor("out", (TOKENS, D), F32, kind="ExternalOutput").ap())
    build(nc, *args)
    r = _run(nc, [arrays], core_ids=[0])
    return r.results[0]["out"].reshape(*a["x"].shape, D)
```

```python
from contextlib import ExitStack

import concourse.bass as bass
import numpy as np
from concourse import mybir

ALU = mybir.AluOpType
ACT = mybir.ActivationFunctionType
AX = mybir.AxisListType
F32 = mybir.dt.float32
I32 = mybir.dt.int32
U32 = mybir.dt.uint32
BF16 = mybir.dt.bfloat16
F16 = mybir.dt.float16

P = 128
D = 128
H = 8
DH = D // H
HALF = D // 2
E = 8
F = 512
FC = F // P
TOKENS = 32 * 128
TIME0, NOTE0, VEL0, DUR0, VOCAB = 128, 378, 410, 418, 668
TIME_STEPS = DUR_STEPS = 250
VEL_BINS = 32
ROWS = VOCAB + 1
TILES = -(-ROWS // P)
LAST = ROWS - (TILES - 1) * P
QUARTER = 32
BIAS_ROWS = 2 * QUARTER + 1
PAIRS = TILES // 2
NOTES_AND_VEL = VEL0 // P
VEL_AT = VEL0 % P
N_VEL = DUR0 - VEL0
EPS = 1e-5
SCALE = DH ** -0.5
BLOCKS = (ROWS - E) // P + E
HEAD_MM = 4
TAIL_MM = 3
BACK_DMA = BLOCKS - TAIL_MM
WIDE = 2 * D + 1
JOBS = TOKENS // P
MM_JOBS = 18
DMA_JOBS = JOBS - MM_JOBS
MM_TOKENS = MM_JOBS * P
DMA_TOKENS = DMA_JOBS * P

TWO_PI_BELOW = 6.283185
ROUND = 1.5 * 2.0 ** 23
PHASE_ROWS = 7
DATA_ROWS = 4


def vocabulary_rows():
    v = np.arange(TILES * P)
    rows = np.zeros((PHASE_ROWS, TILES * P), np.float32)
    time = (v >= TIME0) & (v < NOTE0)
    note = (v >= NOTE0) & (v < VEL0)
    dur = (v >= DUR0) & (v < VOCAB)
    rows[0, time] = (v[time] - TIME0).astype(np.float32) / np.float32(TIME_STEPS)
    rows[1, time] = 1.0
    rows[2, dur] = (v[dur] - DUR0).astype(np.float32) / np.float32(DUR_STEPS)
    rows[3, dur] = 1.0
    rows[4, note] = (v[note] - NOTE0) // 12
    rows[5, note] = (v[note] - NOTE0) % 12
    rows[6, note] = 1.0
    return rows[:, P:]


def pitch_rows():
    i = np.arange(D // 4)
    rows = np.zeros((PHASE_ROWS - DATA_ROWS, D), np.float32)
    rows[0, 0::4] = rows[0, 1::4] = 2.0 ** -i / (2 * np.pi)
    rows[1, 2::4] = rows[1, 3::4] = (i + 1) / 12
    rows[2, 1::2] = 1 / 4
    return rows


def build(nc, x_dma, x_mm, phases, vel, vel_scale, consts, token_emb, weights, rows, w1, w2, b2, out):
    rows_by_expert = nc.dram_tensor("rows_by_expert", [ROWS + P - 1, WIDE], F32)
    row_slots = nc.dram_tensor("row_slots", [P * TILES, 1], U32)
    y_blocks = nc.dram_tensor("y_blocks", [BLOCKS * P, D], F32)
    y_early = nc.dram_tensor("y_early", [BACK_DMA * P + 1, D], F32)
    LOAD_ORDER = (4, 5, 6, 0, 1, 7, 2, 8, 3, *range(9, BLOCKS))
    WEIGHED = {5: (0, 2), 6: (2, 3), 7: (3, 5), 8: (5, 9)}
    WEIGHED.update((b, (b, b + 1)) for b in range(9, BLOCKS))
    EARLY = [(a, b) for a, b in WEIGHED.values() if b <= BACK_DMA]
    TABLE_ORDER = (4, 0, 1, 2, 3, 5)
    BACK_ORDER = (4, 5, 0, 1, 2, 3)
    SINE_TILES = ((1, 2, HALF), (2, 4, 0), (4, 6, HALF))
    PAIR_ORDER = (0, 2, 1)
    with ExitStack() as ctx:
        def sb(name, shape, dt=F32):
            return ctx.enter_context(nc.sbuf_tensor(name, shape, dt))

        def sem(name):
            return ctx.enter_context(nc.semaphore(name))

        tok_in = sb("tok_in", [P, DMA_JOBS], I32)
        mm_in = sb("mm_in", [P, MM_TOKENS], I32)
        ph_in = sb("ph_in", [PHASE_ROWS, (TILES - 1) * P + HALF + D])
        row_basis = ph_in[:, 0:(TILES - 1) * P]
        phase_cols = ph_in[:, (TILES - 1) * P:]
        vel_in = sb("vel_in", [HALF + 1, 2 * P + 2 + N_VEL])
        vel_hid, vel_w2 = vel_in[:, 0:P], vel_in[:, P:2 * P]
        vel_w1, vel_b1 = vel_in[0:HALF, 2 * P:2 * P + 1], vel_in[0:HALF, 2 * P + 1:2 * P + 2]
        vel_n = vel_in[0:HALF, 2 * P + 2:]
        vel_gb = sb("vel_gb", [P, 2, D])
        con = sb("con", [P, 2, P])
        ident, upper = con[:, 0, :], con[:, 1, :]
        w = sb("w", [P, 3 * D + D + E])
        w_proj, w_gate = w[:, 3 * D:4 * D], w[:, 4 * D:]
        w_zv = w[:, D:3 * D]
        rw = sb("rw", [BIAS_ROWS, 3 * D + D + E])
        rest = sb("rest", [BIAS_ROWS, 3 * D + E])
        part = sb("part", [BIAS_ROWS, 3 * D + E], BF16)
        second = sb("second", [BIAS_ROWS, 3 * D + E], BF16)
        bias3 = sb("bias3", [BIAS_ROWS, 3 * D + E], BF16)
        b_zv, b_proj, b_gate = bias3[:, 0:2 * D], bias3[:, 2 * D:3 * D], bias3[:, 3 * D:]
        w1_sb = sb("w1_sb", [P, E, F + FC])
        w2_sb = sb("w2_sb", [P, E, FC, D])
        b2_sb = sb("b2_sb", [P, E, D])
        zeros = sb("zeros", [P, 2 * WIDE], BF16)
        ones = sb("ones", [P, P], F16)
        ones_bf = sb("ones_bf", [P, P], BF16)
        upper_bf = sb("upper_bf", [P, P], BF16)
        neg_half = sb("neg_half", [P, 2])
        tie_rank = sb("tie_rank", [P, E])
        block_no = sb("block_no", [1, BLOCKS])
        row_no = sb("row_no", [P, BLOCKS])
        slot_no = sb("slot_no", [P, HEAD_MM * P])
        h = sb("h", [P, TILES, D])
        turns = sb("turns", [P, TILES, D])
        frac = sb("frac", [P, TILES, D])
        stats = sb("stats", [P, TILES + 1, 6])
        mv = sb("mv", [P, TILES + 1, 2])
        mv2 = sb("mv2", [P, TILES, 2])
        ve = sb("ve", [P, TILES + 1, 1])
        rstd = sb("rstd", [P, TILES + 1, 1])
        rstd2 = sb("rstd2", [P, TILES, 1])
        vn = sb("vn", [P, D])
        attention = sb("attention", [P, 6, TILES, D])
        x1, x1T, hx, zs, att, attT = (attention[:, i] for i in range(6))
        zmax = sb("zmax", [P, TILES, H, 1])
        prob = sb("prob", [P, TILES, D])
        zsum = sb("zsum", [P, TILES, H, 1])
        zrec = sb("zrec", [P, TILES, H, 1])
        pv = sb("pv", [P, TILES, D])
        wide_rows = sb("wide_rows", [P, TILES, WIDE])
        x2, h2, pmax = wide_rows[:, :, 0:D], wide_rows[:, :, D:2 * D], wide_rows[:, :, 2 * D:]
        h2T = sb("h2T", [P, TILES, P])
        center = sb("center", [P, P])
        gate_wb = sb("gate_wb", [P, 2, E])
        logits = sb("logits", [P, TILES, E])
        lmax = sb("lmax", [P, TILES, 1])
        lshift = sb("lshift", [P, TILES, E])
        lexp = sb("lexp", [P, TILES, E])
        lsum = sb("lsum", [P, TILES, 1])
        best = sb("best", [P, TILES, E])
        omax = sb("omax", [P, TILES, 1])
        onehot = sb("onehot", [P, TILES, E], BF16)
        less = sb("less", [P, TILES, E], BF16)
        n_blocks = sb("n_blocks", [P, E])
        nil = sb("nil", [P, E])
        block_start = sb("block_start", [P, 1, E + 1])
        place = sb("place", [P, 2, TILES, E])
        source = sb("source", [P, TILES, 1], U32)
        slot = sb("slot", [P, TILES, 1])
        slot_int = sb("slot_int", [P, TILES, 1], U32)
        slot_back = sb("slot_back", [P, TILES, 1], U32)
        head_pick = sb("head_pick", [P, TILES, HEAD_MM * P])
        diag = sb("diag", [P, TILES, P], F16)
        slot_row = sb("slot_row", [P, ROWS], F16)
        tail_pick = head_pick.rearrange("p t n -> p (t n)")[:, 0:TAIL_MM * ROWS].rearrange("p (i n) -> p i n", n=ROWS)
        ended = sb("ended", [1, BLOCKS, E - 1])
        skipped = sb("skipped", [1, BLOCKS, E - 1])
        padding = sb("padding", [1, 1, E])
        sums = sb("sums", [1, 2, BLOCKS, 1])
        block_expert = sb("block_expert", [1, BLOCKS], I32)
        block_row = sb("block_row", [1, BLOCKS], I32)
        xb = sb("xb", [P, BLOCKS, WIDE])
        xT = sb("xT", [P, 2, P])
        w1_now = sb("w1_now", [P, 3, F + FC])
        act_hid = sb("act_hid", [P, 2, FC, P])
        y = sb("y", [P, BLOCKS, D])
        y_row = sb("y_row", [P, TILES, D])
        tab = sb("tab", [P, TILES, D])
        tab3 = sb("tab3", [P, TILES, 3, D], BF16)
        last3 = sb("last3", [3 * QUARTER, D], BF16)
        last_no = sb("last_no", [3 * QUARTER, 1])
        tok_row = sb("tok_row", [P, DMA_JOBS])
        tok_tile = sb("tok_tile", [P, DMA_JOBS])
        tok = sb("tok", [P, DMA_JOBS], U32)
        tok_slot = sb("tok_slot", [P, DMA_JOBS], U32)
        mm_tok = sb("mm_tok", [P, MM_TOKENS], F16)
        pick = sb("pick", [P, TILES, MM_TOKENS], BF16)
        spent = attention.rearrange("p i t d -> p (i t) d")
        got, made = spent[:, 0:DMA_JOBS], spent[:, DMA_JOBS:JOBS]
        scratch = sb("scratch", [1, 8])

        ps = ctx.enter_context(nc.psum_tensor("ps", [P, 8, 512], F32))
        ps_phase = [ps[:, g, :].rearrange("p (t n) -> p t n", t=2)[:, :, 0:D + HALF] for g in range(PAIRS)]
        ps_vel = ps[:, 4, 0:P]
        ps_zv = [ps[:, g, :].rearrange("p (t k n) -> p t k n", t=2, k=2) for g in range(PAIRS)]
        ps_o = [ps[:, g, 0:2 * P].rearrange("p (t n) -> p t n", n=P) for g in range(PAIRS)]
        ps_turn = [ps[:, PAIRS + g, 0:2 * P].rearrange("p (t n) -> p t n", n=P) for g in range(PAIRS)]
        ps_gate_wb = ps[:, 6, 256:256 + 2 * E].rearrange("p (k e) -> p k e", e=E)
        ps_gate = ps[:, 6, 0:TILES * E].rearrange("p (t e) -> p t e", e=E)
        ps_rank = ps[:, 6, 64:64 + 2 * (TILES + 1) * E].rearrange("p (k t e) -> p k t e", k=2, e=E)
        ps_idle = ps[:, 7, :]
        ps_xT = [ps[:, i, 0:P] for i in (0, 1)]
        ps_hid = [ps[:, i, :].rearrange("p (c n) -> p c n", n=P) for i in (2, 3)]
        ps_y = [ps[:, i, 0:P] for i in (4, 5)]
        ps_slot = ps[:, 6:8, :].rearrange("p b n -> p (b n)")[:, 0:ROWS]
        ps_back = ps[:, 6:8, :].rearrange("p b n -> p (b n)").rearrange("p (t n) -> p t n", n=D)

        phases_in, vel_loaded, scale_in, con_in, emb_in, w_in, rw_in, w1_in, w2_in, b2_in, tok_loaded, mm_loaded = (
            sem(n) for n in ("phases_in", "vel_loaded", "scale_in", "con_in", "emb_in", "w_in", "rw_in", "w1_in",
                             "w2_in", "b2_in", "tok_loaded", "mm_loaded"))
        zeros_set = sem("zeros_set")
        consts_set = sem("consts_set")
        cols_scaled = sem("cols_scaled")
        phases_done = sem("phases_done")
        vel_hidden = sem("vel_hidden")
        vel_out = sem("vel_out")
        frac_done = sem("frac_done")
        sines_done = sem("sines_done")
        dve_seq = sem("dve_seq")
        pool_seq = sem("pool_seq")
        var_done = sem("var_done")
        rstd_done = sem("rstd_done")
        x1_done = sem("x1_done")
        x1T_ps = sem("x1T_ps")
        x1T_done = sem("x1T_done")
        wz_done = sem("wz_done")
        bias_rest = sem("bias_rest")
        bias_part = sem("bias_part")
        bias_second = sem("bias_second")
        bias_done = sem("bias_done")
        head_picks = sem("head_picks")
        diag_done = sem("diag_done")
        slot_row_ps = sem("slot_row_ps")
        tail_picks = sem("tail_picks")
        back_ps = sem("back_ps")
        hx_done = sem("hx_done")
        zv_done = sem("zv_done")
        zs_done = sem("zs_done")
        exp_done = sem("exp_done")
        zsum_done = sem("zsum_done")
        pv_done = sem("pv_done")
        zrec_done = sem("zrec_done")
        att_done = sem("att_done")
        attT_ps = sem("attT_ps")
        attT_done = sem("attT_done")
        o_done = sem("o_done")
        h2_done = sem("h2_done")
        x2_done = sem("x2_done")
        center_done = sem("center_done")
        gate_ready = sem("gate_ready")
        gate_copied = sem("gate_copied")
        h2T_ps = sem("h2T_ps")
        h2T_done = sem("h2T_done")
        gate_done = sem("gate_done")
        lshift_done = sem("lshift_done")
        lexp_done = sem("lexp_done")
        onehot_done = sem("onehot_done")
        upper_done = sem("upper_done")
        less_done = sem("less_done")
        pmax_done = sem("pmax_done")
        rank_done = sem("rank_done")
        source_done = sem("source_done")
        slot_done = sem("slot_done")
        blocks_done = sem("blocks_done")
        slack_out = sem("slack_out")
        rows_sorted = sem("rows_sorted")
        block_in = [sem(f"block_in{b}") for b in range(BLOCKS)]
        xT_ps = sem("xT_ps")
        xT_done = sem("xT_done")
        w1_staged = sem("w1_staged")
        up_done = sem("up_done")
        gelu_done = sem("gelu_done")
        down_done = sem("down_done")
        y_done = sem("y_done")
        y_read = sem("y_read")
        zero_row_out = sem("zero_row_out")
        early_out = sem("early_out")
        y_out = sem("y_out")
        experts_done = sem("experts_done")
        slots_out = sem("slots_out")
        tok_slots = sem("tok_slots")
        y_back = [sem(f"y_back{t}") for t in range(TILES)]
        tab_done = sem("tab_done")
        high_done = sem("high_done")
        rest_done = sem("rest_done")
        mid_done = sem("mid_done")
        low_done = sem("low_done")
        last_done = sem("last_done")
        tok_done = sem("tok_done")
        pick_done = sem("pick_done")
        picked = sem("picked")
        made_done = sem("made_done")
        DMA_PARTS = ((0, 5), (5, 9), (9, DMA_JOBS - 1), (DMA_JOBS - 1, DMA_JOBS))
        rows_got = [sem(f"rows_got{i}") for i in range(len(DMA_PARTS))]
        out_done = sem("out_done")
        MM_BANK = 4
        MM_BANKS = -(-MM_JOBS // MM_BANK)

        ctx.enter_context(nc.allow_low_precision("sums of small whole numbers are exact"))

        def last_rows(t):
            return P if t < TILES - 1 else LAST

        block = ctx.enter_context(nc.Block())

        @block.sync
        def _(sp):
            sp.dma_start(ph_in[:, :], phases[:, :]).then_inc(phases_in, 16)
            sp.dma_start(rw[:, :], rows[:, :]).then_inc(rw_in, 16)
            sp.dma_start(h[:, 0, :], token_emb[:, :]).then_inc(emb_in, 16)
            sp.dma_start(w[:, :], weights[:, :]).then_inc(w_in, 16)
            sp.dma_start(con[:, :, :], consts[:, :, :]).then_inc(con_in, 16)
            sp.dma_start(vel_gb[:, :, :], vel_scale[:, :, :]).then_inc(scale_in, 16)
            sp.dma_start(tok_in[:, :], x_dma[:, :]).then_inc(tok_loaded, 16)
            sp.dma_start(mm_in[:, :], x_mm.broadcast_to([P, MM_TOKENS])).then_inc(mm_loaded, 16)
            sp.dma_start(w1_sb[:, :, :], w1[:, :, :]).then_inc(w1_in, 16)
            sp.dma_start(w2_sb[:, :, :, :], w2[:, :, :, :]).then_inc(w2_in, 16)
            sp.dma_start(b2_sb[:, :, :], b2.broadcast_to([P, E, D])).then_inc(b2_in, 16)
            sp.wait_ge(zeros_set, 1)
            zero_rows = zeros.bitcast(F32)
            sp.dma_start(rows_by_expert.ap()[ROWS:, :], zero_rows[0:P - 1, :]).then_inc(slack_out, 16)
            sp.dma_start(y_early.ap()[BACK_DMA * P:, :], zero_rows[0:1, 0:D]).then_inc(zero_row_out, 16)
            sp.wait_ge(slot_done, 1)
            sp.dma_start(row_slots.rearrange("(p t) n -> p (t n)", p=P), slot_int[:, :, 0]).then_inc(slots_out, 16)
            sp.wait_ge(blocks_done, 1)
            sp.wait_ge(slack_out, 16)
            sp.wait_ge(rows_sorted, TILES * 16)
            for b in LOAD_ORDER:
                a = D if b < HEAD_MM else 0
                row = sp.value_load(block_row[0:1, b:b + 1], min_val=0, max_val=ROWS - 1)
                sp.dma_start(xb[:, b, a:], rows_by_expert.ap()[bass.ds(row, P), a:]).then_inc(block_in[b], 16)
            for a, b in EARLY:
                sp.wait_ge(y_done, b)
                sp.dma_start(y_early.ap()[a * P:b * P, :].rearrange("(b p) n -> p b n", p=P),
                             y[:, a:b, :]).then_inc(early_out, 16)
            sp.dma_start(y_blocks.ap()[0:BACK_DMA * P, :].rearrange("(b p) n -> p b n", p=P),
                         y[:, 0:BACK_DMA, :]).then_inc(y_out, 16)
            for b in range(BACK_DMA, BLOCKS):
                sp.wait_ge(y_done, b + 1)
                sp.dma_start(y_blocks.ap()[b * P:(b + 1) * P, :], y[:, b, :]).then_inc(y_out, 16)
            for c, (a, b) in enumerate(DMA_PARTS):
                sp.wait_ge(rows_got[c], (b - a) * 16)
                sp.dma_start(out[0:DMA_TOKENS, :].rearrange("(p j) n -> p j n", p=P)[:, a:b, :],
                             got[:, a:b, :]).then_inc(out_done, 16)
            sp.wait_ge(out_done, 16 * (len(DMA_PARTS) + MM_BANKS))

        @block.gpsimd
        def _(pool):
            seq = [0]

            def then(ins):
                seq[0] += 1
                ins.then_inc(pool_seq, 1)
                pool.wait_ge(pool_seq, seq[0])

            pool.memset(neg_half[:, :], -0.5)
            pool.memset(ones[:, :], 1.0)
            pool.memset(ones_bf[:, :], 1.0)
            pool.memset(nil[:, :], 0.0)
            pool.memset(onehot[:, TILES - 1, :], 0.0)
            pool.memset(less[:, TILES - 1, :], 0.0)
            pool.memset(block_start[:, 0, 0:1], 0.0)
            pool.iota(tie_rank[:, :], [[-1, E]], base=E, channel_multiplier=0, allow_small_or_imprecise_dtypes=True)
            pool.iota(block_no[:, :], [[1, BLOCKS]], base=0, channel_multiplier=0,
                      allow_small_or_imprecise_dtypes=True)
            pool.iota(slot_no[:, :], [[1, HEAD_MM * P]], base=0, channel_multiplier=0,
                      allow_small_or_imprecise_dtypes=True)
            pool.memset(last3[:, :], 0.0)
            pool.iota(row_no[:, :], [[P, BLOCKS]], base=0, channel_multiplier=1,
                      allow_small_or_imprecise_dtypes=True).then_inc(consts_set, 1)
            pool.wait_ge(consts_set, 1)

            n_var = [0]

            def inverse_root(n, at, m, r):
                n_var[0] += 1
                pool.wait_ge(var_done, n_var[0])
                k = at.stop - at.start
                then(pool.tensor_scalar(ve[0:n, at, 0], m[0:n, at, 1], EPS, 0.0, ALU.add, ALU.add))
                pool.tensor_tensor(r[0:n, at, 0], ve[0:n, at, 0], neg_half[0:n, 0:k], ALU.pow).then_inc(rstd_done, 1)

            def residual(i, g):
                a = slice(2 * g, 2 * g + 2)
                pool.wait_ge(x1_done, i + 1)
                pool.tensor_tensor(hx[:, a, :], h[:, a, :], x1[:, a, :], ALU.add).then_inc(hx_done, 1)

            def pair_root(g, m, r):
                inverse_root(P, slice(2 * g, 2 * g + 2), m, r)

            pair_root(PAIR_ORDER[0], mv, rstd)
            pair_root(PAIR_ORDER[1], mv, rstd)
            inverse_root(HALF, slice(TILES, TILES + 1), mv, rstd)
            residual(0, PAIR_ORDER[0])
            pair_root(PAIR_ORDER[2], mv, rstd)
            residual(1, PAIR_ORDER[1])
            residual(2, PAIR_ORDER[2])
            for g in PAIR_ORDER:
                pair_root(g, mv2, rstd2)
            pool.wait_ge(rstd_done, 2 * PAIRS + 1)
            for t in (2 * PAIR_ORDER[-1], 2 * PAIR_ORDER[-1] + 1):
                ins = pool.tensor_scalar(x2[:, t, :], h2[:, t, :], mv2[:, t, 0:1], rstd2[:, t, :],
                                         ALU.subtract, ALU.mult)
            ins.then_inc(x2_done, 1)
            pool.wait_ge(source_done, 1)
            pool.wait_ge(pmax_done, 1)
            pool.wait_ge(x2_done, PAIRS)
            for t in range(TILES):
                n = last_rows(t)
                pool.indirect_dma_start(
                    out=rows_by_expert.ap()[:, :], out_offset=bass.IndirectOffsetOnAxis(ap=source[0:n, t, :], axis=0),
                    in_=wide_rows[0:n, t, :], in_offset=None).then_inc(rows_sorted, 16)
            pool.wait_ge(tok_done, 1)
            pool.wait_ge(slots_out, 16)
            for j in range(DMA_JOBS):
                pool.indirect_dma_start(
                    out=tok_slot[:, j:j + 1], out_offset=None, in_=row_slots.ap()[:, :],
                    in_offset=bass.IndirectOffsetOnAxis(ap=tok[:, j:j + 1], axis=0)).then_inc(tok_slots, 16)
            pool.wait_ge(zero_row_out, 16)
            pool.wait_ge(early_out, len(EARLY) * 16)
            for t in TABLE_ORDER:
                n = last_rows(t)
                pool.indirect_dma_start(
                    out=y_row[0:n, t, :], out_offset=None, in_=y_early.ap()[:, :],
                    in_offset=bass.IndirectOffsetOnAxis(ap=slot_back[0:n, t, :], axis=0)).then_inc(y_back[t], 16)
            pool.wait_ge(tok_slots, DMA_JOBS * 16)
            pool.wait_ge(y_out, (1 + TAIL_MM) * 16)
            for c, (a, b) in enumerate(DMA_PARTS):
                for j in range(a, b):
                    pool.indirect_dma_start(
                        out=got[:, j, :], out_offset=None, in_=y_blocks.ap()[:, :],
                        in_offset=bass.IndirectOffsetOnAxis(ap=tok_slot[:, j:j + 1], axis=0)).then_inc(rows_got[c], 16)

        @block.scalar
        def _(act):
            act.dma_start(vel_in[:, :], vel[:, :]).then_inc(vel_loaded, 16)
            act.wait_ge(zeros_set, 1)
            act.activation(scratch[:, 0:1], zeros[0:1, 0:1], ACT.Gelu)
            act.wait_ge(vel_loaded, 16)
            act.activation(vel_hid[0:HALF, VEL_AT:VEL_AT + N_VEL], vel_n, ACT.Gelu,
                           bias=vel_b1, scale=vel_w1).then_inc(vel_hidden, 1)
            act.activation(scratch[:, 1:2], zeros[0:1, 0:1], ACT.Sin)

            def sines(i):
                g = PAIR_ORDER[i]
                a, b, c = SINE_TILES[g]
                act.wait_ge(frac_done, i + 1)
                ins = act.activation(h[:, a:b, c:], frac[:, a:b, c:], ACT.Sin, scale=TWO_PI_BELOW)
                if c == HALF:
                    act.wait_ge(phases_done, i + 1)
                    ins = act.activation(h[:, a:b, 0:HALF], ps_phase[g][:, a - 2 * g:, D:], ACT.Copy)
                ins.then_inc(sines_done, 1)

            sines(0)
            act.wait_ge(bias_part, 1)
            act.activation(bias3[0:QUARTER, :], part[0:QUARTER, :], ACT.Copy)
            act.wait_ge(bias_rest, 1)
            act.activation(second[2 * QUARTER:, :], rest[2 * QUARTER:, :], ACT.Copy).then_inc(bias_second, 1)
            sines(1)
            act.activation(bias3[QUARTER:2 * QUARTER, :], rest[QUARTER:2 * QUARTER, :], ACT.Copy).then_inc(bias_done, 1)

            def x1T_copy(i, g):
                act.wait_ge(x1T_ps, i + 1)
                act.activation(x1T[:, 2 * g:2 * g + 2, :], ps_turn[g], ACT.Copy).then_inc(x1T_done, 1)

            def exps(i, g):
                act.wait_ge(zs_done, i + 1)
                act.activation(prob[:, 2 * g:2 * g + 2, :], zs[:, 2 * g:2 * g + 2, :], ACT.Exp,
                               scale=SCALE).then_inc(exp_done, 1)

            def attT_copy(i, g):
                act.wait_ge(attT_ps, i + 1)
                act.activation(attT[:, 2 * g:2 * g + 2, :], ps_turn[g], ACT.Copy).then_inc(attT_done, 1)

            def h2T_copy(i, g):
                act.wait_ge(h2T_ps, i + 1)
                act.activation(h2T[:, 2 * g:2 * g + 2, :], ps_turn[g], ACT.Copy).then_inc(h2T_done, 1)

            x1T_copy(0, PAIR_ORDER[0])
            sines(2)
            act.activation(scratch[:, 2:3], zeros[0:1, 0:1], ACT.Exp)
            for step, i in ((x1T_copy, 1), (exps, 0), (exps, 1), (x1T_copy, 2), (attT_copy, 0), (exps, 2),
                            (attT_copy, 1), (attT_copy, 2), (h2T_copy, 0), (h2T_copy, 1), (h2T_copy, 2)):
                step(i, PAIR_ORDER[i])
            act.wait_ge(lshift_done, 1)
            act.activation(lexp[:, :, :], lshift[:, :, :], ACT.Exp).then_inc(lexp_done, 1)

            def xT_copy(b):
                act.wait_ge(xT_ps, b + 1)
                if b >= 2:
                    act.wait_ge(up_done, b - 1)
                act.activation(xT[:, b % 2, :], ps_xT[b % 2], ACT.Copy).then_inc(xT_done, 1)

            def gelu(b):
                act.wait_ge(up_done, b + 1)
                if b >= 2:
                    act.wait_ge(down_done, b - 1)
                for c in range(FC):
                    act.activation(act_hid[:, b % 2, c, :], ps_hid[b % 2][:, c, :], ACT.Gelu,
                                   bias=w1_now[:, b % 3, F + c:F + c + 1]).then_inc(gelu_done, 1)

            act.activation(scratch[:, 3:4], zeros[0:1, 0:1], ACT.Gelu)
            xT_copy(0)
            for b in range(BLOCKS):
                if b + 1 < BLOCKS:
                    xT_copy(b + 1)
                gelu(b)

            def high(i):
                t = TABLE_ORDER[i]
                n = last_rows(t)
                act.wait_ge(tab_done, i + 1)
                if t == TILES - 1:
                    act.activation(last3[0:n, :], tab[0:n, t, :], ACT.Copy).then_inc(last_done, 1)
                act.activation(tab3[0:n, t, 0, :], tab[0:n, t, :], ACT.Copy).then_inc(high_done, 1)

            def mid(i):
                t = TABLE_ORDER[i]
                n = last_rows(t)
                act.wait_ge(rest_done, i + 1)
                act.activation(tab3[0:n, t, 1, :], tab[0:n, t, :], ACT.Copy).then_inc(mid_done, 1)
                if t == TILES - 1:
                    act.activation(last3[QUARTER:QUARTER + n, :], tab[0:n, t, :], ACT.Copy).then_inc(last_done, 1)

            high(0)
            mid(0)
            high(1)
            for i in range(1, TILES):
                if i + 1 < TILES:
                    high(i + 1)
                mid(i)
            for c in range(MM_BANKS):
                a, b = c * MM_BANK, min(c * MM_BANK + MM_BANK, MM_JOBS)
                act.wait_ge(picked, c + 1)
                act.activation(made[:, a:b, :], ps[:, c, 0:(b - a) * D].rearrange("p (j n) -> p j n", n=D),
                               ACT.Copy).then_inc(made_done, 1)
                act.wait_ge(made_done, c + 1)
                act.dma_start(out[DMA_TOKENS:, :].rearrange("(p j) n -> p j n", p=P)[:, a:b, :],
                              made[:, a:b, :]).then_inc(out_done, 16)

        @block.tensor
        def _(pe):
            def keep_warm(n):
                for _ in range(n):
                    pe.matmul(ps_idle, zeros[:, 0:P], zeros[:, 0:F], start=True, stop=True)

            pe.wait_ge(zeros_set, 1)
            keep_warm(6)
            pe.wait_ge(phases_in, 16)
            pe.wait_ge(cols_scaled, 1)
            for g in PAIR_ORDER:
                a, b, c = SINE_TILES[g]
                for t in range(a, b):
                    mm = pe.matmul(ps_phase[g][:, t - 2 * g, c:], row_basis[:, (t - 1) * P:t * P], phase_cols[:, c:],
                                   start=True, stop=True)
                mm.then_inc(phases_done, 1)
            pe.wait_ge(vel_hidden, 1)
            pe.matmul(ps_vel, vel_hid, vel_w2, start=True, stop=True).then_inc(vel_out, 1)
            keep_warm(4)
            pe.wait_ge(consts_set, 1)
            pe.wait_ge(bias_done, 2)

            def x1_turn(i, g):
                if i == 0:
                    pe.wait_ge(con_in, 16)
                pe.wait_ge(x1_done, i + 1)
                for t in range(2):
                    mm = pe.transpose(ps_turn[g][:, t, :], x1[:, 2 * g + t, :], ident)
                mm.then_inc(x1T_ps, 1)
                bias = b_zv.rearrange("p (t m) -> p t m", t=1)
                pe.matmul(ps_zv[g].rearrange("p t k n -> p t (k n)"), ones_bf[0:BIAS_ROWS, :],
                          bias.broadcast_to([BIAS_ROWS, 2, 2 * D]), start=True, stop=False, skip_group_check=True)

            def scores(i, g):
                if i == 0:
                    pe.wait_ge(wz_done, 1)
                pe.wait_ge(x1T_done, i + 1)
                for t in range(2):
                    mm = pe.matmul(ps_zv[g][:, t, :, :].rearrange("p k n -> p (k n)"), x1T[:, 2 * g + t, :],
                                   w_zv, start=False, stop=True, skip_group_check=True)
                mm.then_inc(zv_done, 1)

            def att_turn(i, g):
                keep_warm(1)
                pe.wait_ge(att_done, i + 1)
                for t in range(2):
                    mm = pe.transpose(ps_turn[g][:, t, :], att[:, 2 * g + t, :], ident)
                mm.then_inc(attT_ps, 1)
                pe.matmul(ps_o[g], ones_bf[0:BIAS_ROWS, :],
                          b_proj.rearrange("p (t n) -> p t n", t=1).broadcast_to([BIAS_ROWS, 2, D]),
                          start=True, stop=False, skip_group_check=True)

            def project(i, g):
                pe.wait_ge(attT_done, i + 1)
                for t in range(2):
                    mm = pe.matmul(ps_o[g][:, t, :], attT[:, 2 * g + t, :], w_proj, start=False, stop=True,
                                   skip_group_check=True)
                mm.then_inc(o_done, 1)

            def h2_turn(i, g):
                keep_warm(1)
                pe.wait_ge(h2_done, i + 1)
                for t in range(2):
                    mm = pe.transpose(ps_turn[g][:, t, :], h2[:, 2 * g + t, :], ident)
                mm.then_inc(h2T_ps, 1)

            def gate(i, g):
                pe.wait_ge(h2T_done, i + 1)
                if i == 0:
                    pe.wait_ge(gate_copied, 1)
                for t in range(2 * g, 2 * g + 2):
                    mm = pe.matmul(ps_gate[:, t, :], h2T[:, t, :], gate_wb[:, 0, :], start=True, stop=True)
                if i == PAIRS - 1:
                    mm.then_inc(gate_done, 1)

            def idle(i, g):
                keep_warm((1, 4)[i])

            def gate_weights(i, g):
                pe.matmul(ps_gate_wb[:, 1, :], ones_bf[0:BIAS_ROWS, :], b_gate, start=True, stop=True)
                pe.wait_ge(w_in, 16)
                pe.wait_ge(center_done, 1)
                pe.matmul(ps_gate_wb[:, 0, :], center[:, :], w_gate, start=True, stop=True).then_inc(gate_ready, 1)

            for step, i in ((x1_turn, 0), (idle, 0), (scores, 0), (x1_turn, 1), (scores, 1), (gate_weights, 0),
                            (idle, 1), (x1_turn, 2), (scores, 2), (att_turn, 0), (project, 0), (att_turn, 1),
                            (project, 1), (att_turn, 2), (h2_turn, 0), (project, 2), (h2_turn, 1), (gate, 0),
                            (h2_turn, 2), (gate, 1), (gate, 2)):
                step(i, PAIR_ORDER[i])
            keep_warm(6)
            pe.wait_ge(onehot_done, 1)
            pe.wait_ge(upper_done, 1)

            def both(ap, n):
                return ap.rearrange("p (k t) e -> p k t e", k=1).broadcast_to([P, 2, n, E])

            pe.matmul(ps_rank[:, :, 0:TILES, :], upper_bf[:, :], both(onehot, TILES), start=True, stop=False,
                      skip_group_check=True)
            for s in range(1, TILES + 1):
                mm = pe.matmul(ps_rank[:, :, s:TILES + 1, :], ones_bf[:, :], both(onehot[:, 0:TILES + 1 - s, :],
                               TILES + 1 - s), start=False, stop=False, skip_group_check=True)
            pe.wait_ge(less_done, 1)
            for s in range(TILES):
                mm = pe.matmul(ps_rank[:, 1, 0:TILES, :], ones_bf[:, :],
                               less[:, s:s + 1, :].broadcast_to([P, TILES, E]), start=False, stop=(s == TILES - 1),
                               skip_group_check=True)
            mm.then_inc(rank_done, 1)
            pe.wait_ge(w2_in, 16)

            def turn(b):
                if b >= 2:
                    pe.wait_ge(xT_done, b - 1)
                if b < HEAD_MM:
                    for t in range(TILES):
                        n = last_rows(t)
                        pe.wait_ge(head_picks, min(b, 2) * TILES + t + 1)
                        mm = pe.matmul(ps_xT[b % 2], x2[0:n, t, :], head_pick[0:n, t, b * P:(b + 1) * P],
                                       start=(t == 0), stop=(t == TILES - 1))
                    mm.then_inc(xT_ps, 1)
                else:
                    pe.wait_ge(block_in[b], 16)
                    pe.transpose(ps_xT[b % 2], xb[:, b, 0:D], ident).then_inc(xT_ps, 1)

            def up(b):
                pe.wait_ge(w1_staged, b + 1)
                pe.wait_ge(xT_done, b + 1)
                if b >= 2:
                    pe.wait_ge(gelu_done, FC * (b - 1))
                for c in range(FC):
                    mm = pe.matmul(ps_hid[b % 2][:, c, :], w1_now[:, b % 3, c * P:(c + 1) * P], xT[:, b % 2, :],
                                   start=True, stop=True)
                mm.then_inc(up_done, 1)

            def down(b, e):
                if b >= 2:
                    pe.wait_ge(y_read, b - 1)
                for c in range(FC):
                    pe.wait_ge(gelu_done, FC * b + c + 1)
                    mm = pe.matmul(ps_y[b % 2], act_hid[:, b % 2, c, :], w2_sb[:, bass.ds(e, 1), c, :],
                                   start=(c == 0), stop=(c == FC - 1))
                mm.then_inc(down_done, 1)

            def spread_slots():
                pe.wait_ge(diag_done, 1)
                across = diag.rearrange("p t n -> p (t n)")
                for a, b in ((0, 512), (512, ROWS)):
                    mm = pe.matmul(ps_slot[:, a:b], ones[:, :], across[:, a:b], start=True, stop=True)
                mm.then_inc(slot_row_ps, 1)

            def back(b):
                pe.wait_ge(y_done, b + 1)
                pe.wait_ge(tail_picks, 1 + TAIL_MM)
                for t in BACK_ORDER:
                    n = last_rows(t)
                    mm = pe.matmul(ps_back[0:n, t, :], tail_pick[:, b - BACK_DMA, t * P:t * P + n], y[:, b, :],
                                   start=(b == BACK_DMA and t % 4 == 0), stop=(b == BLOCKS - 1),
                                   skip_group_check=True)
                    if b == BLOCKS - 1 and t in (3, TILES - 1):
                        mm.then_inc(back_ps, 1)

            keep_warm(8)
            pe.wait_ge(x2_done, PAIRS)
            turn(0)
            turn(1)
            pe.wait_ge(experts_done, 1)
            up(0)
            for b in range(BLOCKS):
                e = pe.value_load(block_expert[0:1, b:b + 1], min_val=0, max_val=E - 1)
                if b + 1 < BLOCKS:
                    up(b + 1)
                if b + 2 < BLOCKS:
                    turn(b + 2)
                down(b, e)
                if b == 1:
                    spread_slots()
            for b in range(BACK_DMA, BLOCKS):
                back(b)
            for banks in ((0, 1),) + tuple((c,) for c in range(2, MM_BANKS)):
                for i, t in enumerate(TABLE_ORDER):
                    if banks[0] == 0:
                        pe.wait_ge(pick_done, i + 1)
                    last = t == TILES - 1
                    for k in range(1 if last else 3):
                        if banks[0] == 0 and last:
                            pe.wait_ge(last_done, 2)
                        if banks[0] == 0:
                            pe.wait_ge((high_done, mid_done, low_done)[2 if last else k], i + 1)
                        for c in banks:
                            for j in range(c * MM_BANK, min(c * MM_BANK + MM_BANK, MM_JOBS)):
                                tokens = slice(j * P, (j + 1) * P)
                                mm = pe.matmul(ps[:, c, (j % MM_BANK) * D:(j % MM_BANK + 1) * D],
                                               pick[0:3 * QUARTER, t, tokens] if last else pick[:, t, tokens],
                                               last3[:, :] if last else tab3[:, t, k, :],
                                               start=(i == 0 and k == 0 and j % MM_BANK == 0),
                                               stop=last, skip_group_check=True)
                            if last:
                                mm.then_inc(picked, 1)

        @block.vector
        def _(dve):
            seq = [0]

            def then(ins):
                seq[0] += 1
                ins.then_inc(dve_seq, 1)
                dve.wait_ge(dve_seq, seq[0])

            def tick(ins):
                seq[0] += 1
                ins.then_inc(dve_seq, 1)
                return seq[0]

            def after(n):
                dve.wait_ge(dve_seq, n)

            n_root = [0]

            def root_ready():
                n_root[0] += 1
                dve.wait_ge(rstd_done, n_root[0])

            dve.memset(zeros[:, :].bitcast(U32), 0).then_inc(zeros_set, 1)
            dve.wait_ge(phases_in, 16)
            dve.tensor_scalar(phase_cols[0:DATA_ROWS, 0:D], phase_cols[0:DATA_ROWS, 0:D], float(1 / (2 * np.pi)), None,
                              ALU.mult).then_inc(cols_scaled, 1)

            def fraction(i):
                g = PAIR_ORDER[i]
                a, b, c = SINE_TILES[g]
                phase = ps_phase[g][:, a - 2 * g:, c:D]
                dve.wait_ge(phases_done, i + 1)
                then(dve.tensor_scalar(turns[:, a:b, c:], phase, ROUND, ROUND, ALU.add, ALU.subtract))
                dve.tensor_tensor(frac[:, a:b, c:], phase, turns[:, a:b, c:], ALU.subtract).then_inc(frac_done, 1)

            def stat(src, m, g):
                for t in (2 * g, 2 * g + 1):
                    ins = dve.bn_stats(stats[:, t, :], src[:, t, :])
                then(ins)
                for t in (2 * g, 2 * g + 1):
                    ins = dve.bn_aggr(m[:, t, :], stats[:, t, :])
                ins.then_inc(var_done, 1)

            def norm(src, m, r, dst, done, g):
                for t in (2 * g, 2 * g + 1):
                    ins = dve.tensor_scalar(dst[:, t, :], src[:, t, :], m[:, t, 0:1], r[:, t, :],
                                            ALU.subtract, ALU.mult)
                ins.then_inc(done, 1)

            def stat1(i, g):
                stat(h, mv, g)

            def norm1(i, g):
                root_ready()
                norm(h, mv, rstd, x1, x1_done, g)

            def heads(ap):
                return ap.rearrange("p t (h d) -> p t h d", d=DH)

            def wide(ap):
                return ap.broadcast_to([P, 2, H, DH])

            def shift(i, g):
                a = slice(2 * g, 2 * g + 2)
                dve.wait_ge(zv_done, i + 1)
                z = heads(ps_zv[g][:, :, 0, :])
                then(dve.tensor_reduce(zmax[:, a, :, :], z, AX.X, ALU.max))
                dve.tensor_tensor(heads(zs[:, a, :]), z, wide(zmax[:, a, :, :]), ALU.subtract).then_inc(zs_done, 1)

            def weigh(i, g):
                a = slice(2 * g, 2 * g + 2)
                dve.wait_ge(exp_done, i + 1)
                dve.tensor_reduce(zsum[:, a, :, :], heads(prob[:, a, :]), AX.X, ALU.add).then_inc(zsum_done, 1)
                dve.tensor_tensor(pv[:, a, :], prob[:, a, :], ps_zv[g][:, :, 1, :], ALU.mult).then_inc(pv_done, 1)

            def share(i, g):
                a = slice(2 * g, 2 * g + 2)
                dve.wait_ge(zsum_done, i + 1)
                dve.reciprocal(zrec[:, a, :, :], zsum[:, a, :, :]).then_inc(zrec_done, 1)
                dve.wait_ge(pv_done, i + 1)
                dve.wait_ge(zrec_done, i + 1)
                dve.tensor_tensor(heads(att[:, a, :]), heads(pv[:, a, :]), wide(zrec[:, a, :, :]),
                                  ALU.mult).then_inc(att_done, 1)

            def stat2(i, g):
                dve.wait_ge(o_done, i + 1)
                dve.wait_ge(hx_done, i + 1)
                a = slice(2 * g, 2 * g + 2)
                dve.tensor_tensor(h2[:, a, :], hx[:, a, :], ps_o[g], ALU.add).then_inc(h2_done, 1)
                dve.wait_ge(h2_done, i + 1)
                stat(h2, mv2, g)

            def norm2(i, g):
                root_ready()
                norm(h2, mv2, rstd2, x2, x2_done, g)

            dve.wait_ge(rw_in, 16)
            then(dve.tensor_tensor(rw[:, D:2 * D], rw[:, 0:D], rw[:, D:2 * D], ALU.subtract))
            row = rw[:, D:]
            dve.tensor_copy(part[:, :], row).then_inc(bias_part, 1)
            fraction(0)
            dve.wait_ge(bias_part, 1)
            dve.tensor_tensor(rest[:, :], row, part[:, :], ALU.subtract).then_inc(bias_rest, 1)
            fraction(1)
            dve.wait_ge(sines_done, 1)
            dve.wait_ge(emb_in, 16)
            stat1(0, PAIR_ORDER[0])
            dve.wait_ge(bias_second, 1)
            dve.tensor_tensor(bias3[2 * QUARTER:, :], rest[2 * QUARTER:, :], second[2 * QUARTER:, :],
                              ALU.subtract).then_inc(bias_done, 1)
            dve.wait_ge(sines_done, 2)
            stat1(1, PAIR_ORDER[1])
            norm1(0, PAIR_ORDER[0])
            dve.wait_ge(w_in, 16)
            dve.tensor_tensor(w[:, D:2 * D], w[:, 0:D], w[:, D:2 * D], ALU.subtract).then_inc(wz_done, 1)
            fraction(2)
            n = HALF
            dve.wait_ge(vel_out, 1)
            then(dve.bn_stats(stats[0:n, TILES, :], ps_vel[0:n, :]))
            dve.bn_aggr(mv[0:n, TILES, :], stats[0:n, TILES, :]).then_inc(var_done, 1)
            g = PAIR_ORDER[2]
            dve.wait_ge(sines_done, 3)
            then(dve.tensor_tensor(h[:, 2 * g:2 * g + 2, 0:HALF], h[:, 2 * g:2 * g + 2, 0:HALF],
                                   ps_phase[g][:, :, D:], ALU.add))
            norm1(1, PAIR_ORDER[1])
            root_ready()
            then(dve.tensor_scalar(vn[0:n, :], ps_vel[0:n, :], mv[0:n, TILES, 0:1], rstd[0:n, TILES, :],
                                   ALU.subtract, ALU.mult))
            shift(0, PAIR_ORDER[0])
            dve.wait_ge(scale_in, 16)
            then(dve.tensor_tensor(vn[0:n, :], vn[0:n, :], vel_gb[0:n, 0, :], ALU.mult))
            then(dve.tensor_tensor(vn[0:n, :], vn[0:n, :], vel_gb[0:n, 1, :], ALU.add))
            t = NOTES_AND_VEL
            then(dve.tensor_tensor(h[0:n, t, :], h[0:n, t, :], vn[0:n, :], ALU.add))
            stat1(2, PAIR_ORDER[2])
            dve.wait_ge(con_in, 16)
            dve.tensor_scalar(center[:, :], ident, -1 / D, None, ALU.add).then_inc(center_done, 1)

            def gate_copy(i, g):
                dve.wait_ge(gate_ready, 1)
                dve.tensor_copy(gate_wb[:, :, :], ps_gate_wb).then_inc(gate_copied, 1)

            for step, i in ((shift, 1), (norm1, 2), (weigh, 0), (share, 0), (weigh, 1), (shift, 2), (share, 1),
                            (gate_copy, 0), (weigh, 2), (share, 2),
                            (stat2, 0), (stat2, 1), (stat2, 2), (norm2, 0), (norm2, 1)):
                step(i, PAIR_ORDER[i])
            dve.tensor_copy(upper_bf[:, :], upper).then_inc(upper_done, 1)
            root_ready()
            dve.wait_ge(gate_done, 1)
            then(dve.tensor_tensor(logits[:, :, :], ps_gate, rstd2[:, :, :].broadcast_to([P, TILES, E]), ALU.mult))
            then(dve.tensor_tensor(logits[:, :, :], logits[:, :, :],
                                   gate_wb[:, 1:2, :].broadcast_to([P, TILES, E]), ALU.add))
            then(dve.tensor_reduce(lmax[:, :, :], logits[:, :, :], AX.X, ALU.max))
            wide_max = lmax[:, :, :].broadcast_to([P, TILES, E])
            then(dve.tensor_tensor(best[:, :, :], logits[:, :, :], wide_max, ALU.is_equal))
            dve.tensor_tensor(lshift[:, :, :], logits[:, :, :], wide_max, ALU.subtract).then_inc(lshift_done, 1)
            dve.wait_ge(consts_set, 1)
            then(dve.tensor_tensor(best[:, :, :], best[:, :, :],
                                   tie_rank.rearrange("p (a e) -> p a e", a=1).broadcast_to([P, TILES, E]), ALU.mult))
            then(dve.tensor_reduce(omax[:, :, :], best[:, :, :], AX.X, ALU.max))
            for dst, src, op, done in ((onehot, best, ALU.is_equal, onehot_done),
                                       (less, tie_rank.rearrange("p (a e) -> p a e", a=1).broadcast_to([P, TILES, E]),
                                        ALU.is_lt, less_done)):
                for a, b, n in ((0, TILES - 1, P), (TILES - 1, TILES, LAST)):
                    ins = dve.tensor_tensor(dst[0:n, a:b, :], src[0:n, a:b, :],
                                            omax[0:n, a:b, :].broadcast_to([n, b - a, E]), op)
                ins.then_inc(done, 1)
            dve.wait_ge(lexp_done, 1)
            then(dve.tensor_reduce(lsum[:, :, :], lexp[:, :, :], AX.X, ALU.add))
            dve.reciprocal(pmax[:, :, :], lsum[:, :, :]).then_inc(pmax_done, 1)
            dve.wait_ge(rank_done, 1)
            total = ps_rank[:, 0, TILES, :]
            rounded = tick(dve.tensor_scalar(n_blocks[:, :], total, (P - 1) / 2, 1 / P, ALU.add, ALU.mult))
            placed = tick(dve.tensor_tensor(place[:, 1, :, :], ps_rank[:, 1, 0:TILES, :], onehot[:, :, :], ALU.mult))
            after(rounded)
            rounded = tick(dve.tensor_scalar(n_blocks[:, :], n_blocks[:, :], ROUND, ROUND, ALU.add, ALU.subtract))
            after(placed)
            dve.tensor_reduce(source[:, :, :], place[:, 1, :, :], AX.X, ALU.add).then_inc(source_done, 1)
            after(rounded)
            then(dve.tensor_tensor_scan(block_start[:, 0, 1:], n_blocks[:, :], nil[:, :], 0.0, ALU.add, ALU.add))
            placed = tick(dve.scalar_tensor_tensor(
                place[:, 0, :, :], block_start[:, :, 0:E].broadcast_to([P, TILES, E]), float(P),
                ps_rank[:, 0, 0:TILES, :], ALU.mult, ALU.add))
            grid = [1, BLOCKS, E - 1]
            number = block_no.rearrange("p (b e) -> p b e", e=1)
            compared = tick(dve.tensor_tensor(ended[:, :, :], number.broadcast_to(grid),
                                              block_start[0:1, :, 1:E].broadcast_to(grid), ALU.is_ge))
            after(placed)
            placed = tick(dve.tensor_tensor(place[:, 0, :, :], place[:, 0, :, :], onehot[:, :, :], ALU.mult))
            after(compared)
            dve.tensor_reduce(block_expert.rearrange("p (b e) -> p b e", e=1), ended[:, :, :], AX.X, ALU.add
                              ).then_inc(experts_done, 1)
            after(placed)
            then(dve.tensor_reduce(slot[:, :, :], place[:, 0, :, :], AX.X, ALU.add))

            def head_picking(a, b):
                for t in range(TILES):
                    dve.tensor_scalar(head_pick[:, t, a * P:b * P], slot_no[:, a * P:b * P], slot[:, t, :], None,
                                      ALU.is_equal).then_inc(head_picks, 1)

            dve.wait_ge(experts_done, 1)
            dve.wait_ge(w1_in, 16)
            dve.wait_ge(b2_in, 16)

            def expert(b):
                return dve.value_load(block_expert[0:1, b:b + 1], min_val=0, max_val=E - 1)

            def stage(b, e):
                if b >= 3:
                    dve.wait_ge(up_done, b - 2)
                    dve.wait_ge(gelu_done, FC * (b - 2))
                dve.tensor_copy(w1_now[:, b % 3, :], w1_sb[:, bass.ds(e, 1), :].rearrange("p a n -> p (a n)")
                                ).then_inc(w1_staged, 1)

            def add_bias(b, e):
                dve.wait_ge(down_done, b + 1)
                dve.tensor_tensor(y[:, b, :], ps_y[b % 2], b2_sb[:, bass.ds(e, 1), :].rearrange("p a n -> p (a n)"),
                                  ALU.add).then_inc(y_read, 1)

            def weigh_and_add(b):
                dve.wait_ge(y_read, b + 1)
                dve.wait_ge(block_in[b], 16)
                dve.scalar_tensor_tensor(y[:, b, :], y[:, b, :], xb[:, b, 2 * D:], xb[:, b, D:2 * D],
                                         ALU.mult, ALU.add).then_inc(y_done, 1)

            head_picking(0, 1)
            experts = [expert(0)]
            stage(0, experts[0])
            head_picking(1, 2)
            experts.append(expert(1))
            stage(1, experts[1])
            experts.append(expert(2))
            stage(2, experts[2])
            dve.tensor_copy(slot_int[:, :, :], slot[:, :, :])
            dve.tensor_scalar(slot_back[:, :, :], slot[:, :, :], float(BACK_DMA * P), None, ALU.min
                              ).then_inc(slot_done, 1)
            then(dve.scalar_tensor_tensor(padding[:, 0, :], n_blocks[0:1, :], -float(P), ps_rank[0:1, 0, TILES, :],
                                          ALU.mult, ALU.add))
            then(dve.tensor_tensor(skipped[:, :, :], ended[:, :, :], padding[:, :, 0:E - 1].broadcast_to(grid),
                                   ALU.mult))
            then(dve.tensor_reduce(sums[:, 0, :, :], skipped[:, :, :], AX.X, ALU.add))
            then(dve.scalar_tensor_tensor(sums[:, 1, :, :], number, float(P), sums[:, 0, :, :], ALU.mult, ALU.add))
            dve.tensor_scalar(block_row[:, :], sums[:, 1, :, 0], float(ROWS - 1), None, ALU.min
                              ).then_inc(blocks_done, 1)
            head_picking(2, HEAD_MM)
            experts.append(expert(3))
            dve.wait_ge(tok_loaded, 16)
            then(dve.tensor_scalar(tok_row[:, :], tok_in[:, :], float(VOCAB), 0.0, ALU.min, ALU.max))
            then(dve.tensor_scalar(tok_tile[:, :], tok_row[:, :], -(P - 1) / 2, 1 / P, ALU.add, ALU.mult))
            then(dve.tensor_scalar(tok_tile[:, :], tok_tile[:, :], ROUND, ROUND, ALU.add, ALU.subtract))
            then(dve.tensor_scalar(tok_row[:, :], tok_row[:, :], float(TILES), None, ALU.mult))
            dve.scalar_tensor_tensor(tok[:, :], tok_tile[:, :], float(1 - P * TILES), tok_row[:, :],
                                     ALU.mult, ALU.add).then_inc(tok_done, 1)

            def slots_diagonal():
                for t in range(TILES):
                    ins = dve.tensor_scalar(diag[:, t, :], ident, slot[:, t, :], None, ALU.mult)
                ins.then_inc(diag_done, 1)

            def clip_tokens():
                for k in range(3):
                    at = slice(k * QUARTER, (k + 1) * QUARTER)
                    dve.tensor_scalar(last_no[at, :], row_no[at, TILES - 1:TILES], float(-k * QUARTER), None, ALU.add)
                dve.wait_ge(mm_loaded, 16)
                then(dve.tensor_scalar(mm_tok[:, :], mm_in[:, :], float(VOCAB), 0.0, ALU.min, ALU.max))

            def copy_slots():
                dve.wait_ge(slot_row_ps, 1)
                dve.tensor_copy(slot_row[:, :], ps_slot).then_inc(tail_picks, 1)

            def tail_picking(i):
                if i == 0:
                    dve.wait_ge(tail_picks, 1)
                    dve.wait_ge(xT_ps, HEAD_MM)
                dve.tensor_scalar(tail_pick[:, i, :], slot_row[:, :], row_no[:, BACK_DMA + i:BACK_DMA + i + 1], None,
                                  ALU.is_equal).then_inc(tail_picks, 1)

            def picking(t):
                n, number = (P, row_no[:, t:t + 1]) if t < TILES - 1 else (3 * QUARTER, last_no[:, :])
                dve.tensor_scalar(pick[0:n, t, :], mm_tok[0:n, :], number, None, ALU.is_equal).then_inc(pick_done, 1)

            def spare(b):
                if b == 0:
                    slots_diagonal()
                elif b == 1:
                    clip_tokens()
                    picking(TABLE_ORDER[0])
                elif b == 2:
                    copy_slots()
                    tail_picking(0)
                elif b == 3:
                    for i in range(1, TAIL_MM):
                        tail_picking(i)
                elif b < 2 + TILES:
                    picking(TABLE_ORDER[b - 3])
                elif b == BACK_DMA:
                    picking(TABLE_ORDER[-1])

            for b in range(BLOCKS):
                if b + 4 < BLOCKS:
                    experts.append(expert(b + 4))
                if b + 3 < BLOCKS and b != BACK_DMA - 1:
                    stage(b + 3, experts[b + 3])
                add_bias(b, experts[b])
                for k in range(*WEIGHED.get(b, (0, 0))):
                    weigh_and_add(k)
                if b + 3 < BLOCKS and b == BACK_DMA - 1:
                    stage(b + 3, experts[b + 3])
                spare(b)

            def join(i):
                t = TABLE_ORDER[i]
                n = last_rows(t)
                dve.wait_ge(back_ps, 1 if t >= 4 else 2)
                dve.wait_ge(y_back[t], 16)
                dve.tensor_tensor(tab[0:n, t, :], ps_back[0:n, t, :], y_row[0:n, t, :], ALU.add).then_inc(tab_done, 1)

            def rest_of(i):
                t = TABLE_ORDER[i]
                n = last_rows(t)
                dve.wait_ge(high_done, i + 1)
                dve.tensor_tensor(tab[0:n, t, :], tab[0:n, t, :], tab3[0:n, t, 0, :], ALU.subtract
                                  ).then_inc(rest_done, 1)

            def low(i):
                t = TABLE_ORDER[i]
                n = last_rows(t)
                dve.wait_ge(mid_done, i + 1)
                dst = tab3[:, t, 2, :] if t < TILES - 1 else last3[2 * QUARTER:2 * QUARTER + n, :]
                dve.tensor_tensor(dst, tab[0:n, t, :], tab3[0:n, t, 1, :], ALU.subtract).then_inc(low_done, 1)

            join(0)
            rest_of(0)
            low(0)
            join(1)
            for i in range(1, TILES + 1):
                if i + 1 < TILES:
                    join(i + 1)
                if i < TILES:
                    rest_of(i)
                if i >= 2:
                    low(i - 1)


def kernel(**inputs):
    import numpy as _np
    import concourse.bacc as _bacc
    from concourse.bass_utils import run_bass_kernel_spmd as _run

    a = {k.removeprefix("L0_"): _np.asarray(v) for k, v in inputs.items()}
    f32 = _np.float32
    x = a["x"].reshape(-1)

    sines = _np.zeros((PHASE_ROWS, D + HALF), f32)
    for k, name in enumerate(("time_lin_w", "time_lin_b", "dur_lin_w", "dur_lin_b")):
        sines[k, D:] = a["tok_" + name]
    for k, name in enumerate(("time_w", "time_b", "dur_w", "dur_b")):
        sines[k, HALF:D] = a["tok_" + name]
    sines[4:, 0:D] = pitch_rows()

    vel = _np.zeros((HALF + 1, 2 * P + 2 + N_VEL), f32)
    vel[HALF, VEL_AT:VEL_AT + N_VEL] = 1.0
    vel[0:HALF, P:2 * P] = a["tok_vel_w2"].T
    vel[HALF, P:2 * P] = a["tok_vel_b2"]
    vel[0:HALF, 2 * P] = a["tok_vel_w1"]
    vel[0:HALF, 2 * P + 1] = a["tok_vel_b1"]
    vel[:, 2 * P + 2:] = _np.arange(N_VEL, dtype=f32) / f32(VEL_BINS)
    vel_scale = _np.zeros((P, 2, D), f32)
    vel_scale[VEL_AT:VEL_AT + N_VEL, 0] = a["tok_vel_ln_g"]
    vel_scale[VEL_AT:VEL_AT + N_VEL, 1] = a["tok_vel_ln_b"]

    w1 = _np.zeros((P, E, F + FC), f32)
    w1[:, :, 0:F] = a["ffn_W1"].transpose(1, 0, 2)
    w1[:, :, F:] = a["ffn_b1"].reshape(E, FC, P).transpose(2, 0, 1)
    rows = _np.zeros((BIAS_ROWS, 3 * D + D + E), f32)
    rows[0::QUARTER] = _np.concatenate([a["attn_b_qkv"], a["attn_b_proj"], a["ffn_bs"]])
    arrays = {
        "x_dma": x[:DMA_TOKENS].reshape(P, DMA_JOBS),
        "x_mm": x[DMA_TOKENS:].reshape(P, MM_JOBS).T.reshape(1, MM_TOKENS),
        "phases": _np.concatenate([vocabulary_rows(), sines], 1),
        "vel": vel,
        "vel_scale": vel_scale,
        "consts": _np.stack([_np.eye(P, dtype=f32), _np.triu(_np.ones((P, P), f32), 1)], 1),
        "token_emb": a["tok_token_emb"],
        "weights": _np.concatenate([a["attn_W_qkv"], a["attn_W_proj"], a["ffn_Ws"]], 1),
        "rows": rows,
        "w1": w1,
        "w2": a["ffn_W2"].reshape(E, FC, P, D).transpose(2, 0, 1, 3),
        "b2": a["ffn_b2"][None],
    }
    nc = _bacc.Bacc("TRN2", target_bir_lowering=False, num_devices=1)
    args = []
    for name in arrays:
        arrays[name] = _np.ascontiguousarray(arrays[name])
        args.append(nc.dram_tensor(name, arrays[name].shape, mybir.dt.from_np(arrays[name].dtype),
                                   kind="ExternalInput").ap())
    args.append(nc.dram_tensor("out", (TOKENS, D), F32, kind="ExternalOutput").ap())
    build(nc, *args)
    r = _run(nc, [arrays], core_ids=[0])
    return r.results[0]["out"].reshape(*a["x"].shape, D)
```
